# Optimizing a Trainium2 kernel written in Bass

```python
import numpy as np
import jax
import jax.numpy as jnp

def _softmax(x, axis=-1):
    return jax.nn.softmax(x, axis=axis)

def _gelu(x):
    return jax.nn.gelu(x, approximate=True)

def _silu(x):
    return jax.nn.silu(x)

def _sigmoid(x):
    return jax.nn.sigmoid(x)

def _layernorm(x, axis=-1, eps=1e-05):
    m = jnp.mean(x, axis=axis, keepdims=True)
    v = jnp.var(x, axis=axis, keepdims=True)
    return (x - m) / jnp.sqrt(v + eps)

def _scatter_add(tgt, idx, src, axis=0):
    return tgt.at[idx].add(src)

def _segment_sum(src, seg, n):
    return jax.ops.segment_sum(src, seg, n)
kernel_name = 'mk_macaron_d1_jaxref_r2_dce682'

def setup_inputs(seed: int=0):
    np.random.seed(seed)
    _w = jnp.asarray

    def _L0_attn_setup():
        import jax, jax.numpy as jnp
        import numpy as np
        import math
        D_MODEL = 1024
        D_STATE = 16
        EXPAND = 2
        D_INNER = D_MODEL * EXPAND
        DT_RANK = math.ceil(D_MODEL / 16)
        BATCH, SEQ_LEN = (2, 256)
        key = jax.random.key(seed)
        ks = jax.random.split(key, 6)
        x = jax.random.normal(ks[0], (BATCH, SEQ_LEN, D_INNER), dtype=jnp.float32)
        A_log = jnp.log(jax.random.uniform(ks[1], (D_INNER, D_STATE), minval=0.5, maxval=16.0, dtype=jnp.float32))
        D = jnp.ones((D_INNER,), dtype=jnp.float32)
        x_proj_w = 0.02 * jax.random.normal(ks[2], (DT_RANK + 2 * D_STATE, D_INNER), dtype=jnp.float32)
        dt_init_std = DT_RANK ** (-0.5)
        dt_proj_w = jax.random.uniform(ks[3], (D_INNER, DT_RANK), minval=-dt_init_std, maxval=dt_init_std, dtype=jnp.float32)
        dt = jnp.exp(jax.random.uniform(ks[4], (D_INNER,), dtype=jnp.float32) * (math.log(0.1) - math.log(0.001)) + math.log(0.001))
        dt = jnp.clip(dt, 0.0001, None)
        dt_proj_b = dt + jnp.log(-jnp.expm1(-dt))
        return {'x': x, 'A_log': A_log, 'D': D, 'x_proj_w': x_proj_w, 'dt_proj_w': dt_proj_w, 'dt_proj_b': dt_proj_b}
    _L0_attn_in = _L0_attn_setup()

    def _L0_ffn_setup():
        import jax, jax.numpy as jnp
        import numpy as np
        N_STREAMS = 4
        DIM = 512
        SINKHORN_ITERS = 50
        SINKHORN_TAU = 0.1
        RMS_EPS = 1.1920929e-07

        def sinkhorn_log(logits, num_iters=SINKHORN_ITERS, tau=SINKHORN_TAU):
            Z = logits / tau
            u0 = jnp.zeros(Z.shape[:-1], Z.dtype)
            v0 = jnp.zeros_like(u0)

            def step(carry, _):
                u, v = carry
                u = -jax.nn.logsumexp(Z + v[..., None, :], axis=-1)
                v = -jax.nn.logsumexp(Z + u[..., :, None], axis=-2)
                return ((u, v), None)
            (u, v), _ = jax.lax.scan(step, (u0, v0), None, length=num_iters)
            return jnp.exp(Z + u[..., :, None] + v[..., None, :])
        key = jax.random.key(seed)
        ks = jax.random.split(key, 6)
        B, T = (4, 1024)
        n, C = (N_STREAMS, DIM)
        wd = n * C
        x = jax.random.normal(ks[0], (B, T, wd), dtype=jnp.float32)
        W_res = 0.01 * jax.random.normal(ks[1], (n * n, wd), dtype=jnp.float32)
        W_pre = 0.01 * jax.random.normal(ks[2], (n, wd), dtype=jnp.float32)
        W_post = 0.01 * jax.random.normal(ks[3], (n, wd), dtype=jnp.float32)
        H_res_base = jnp.full((n, n), -0.5, dtype=jnp.float32)
        H_res_base = H_res_base.at[jnp.arange(n), jnp.arange(n)].set(0.0)
        H_pre_base = jnp.zeros((n,), dtype=jnp.float32).at[0].set(1.0)
        H_post_base = jnp.zeros((n,), dtype=jnp.float32)
        gate = jnp.array([5.0], dtype=jnp.float32)
        W_branch = 1.0 / np.sqrt(C) * jax.random.normal(ks[4], (C, C), dtype=jnp.float32)
        return {'x': x, 'W_res': W_res, 'W_pre': W_pre, 'W_post': W_post, 'H_res_base': H_res_base, 'H_pre_base': H_pre_base, 'H_post_base': H_post_base, 'gate': gate, 'W_branch': W_branch}
    _L0_ffn_in = _L0_ffn_setup()
    _d = {'L0_attn_x': _L0_attn_in['x'], 'L0_attn_A_log': _L0_attn_in['A_log'], 'L0_attn_D': _L0_attn_in['D'], 'L0_attn_x_proj_w': _L0_attn_in['x_proj_w'], 'L0_attn_dt_proj_w': _L0_attn_in['dt_proj_w'], 'L0_attn_dt_proj_b': _L0_attn_in['dt_proj_b'], 'L0_ffn_W_res': _L0_ffn_in['W_res'], 'L0_ffn_W_pre': _L0_ffn_in['W_pre'], 'L0_ffn_W_post': _L0_ffn_in['W_post'], 'L0_ffn_H_res_base': _L0_ffn_in['H_res_base'], 'L0_ffn_H_pre_base': _L0_ffn_in['H_pre_base'], 'L0_ffn_H_post_base': _L0_ffn_in['H_post_base'], 'L0_ffn_gate': _L0_ffn_in['gate'], 'L0_ffn_W_branch': _L0_ffn_in['W_branch']}
    _x0 = _d['L0_attn_x']
    _d['L0_attn_x'] = jax.random.normal(jax.random.fold_in(jax.random.key(seed), 1), (2, 2048, 2048), dtype=_x0.dtype)
    del _x0
    return _d

def reference(L0_attn_x, L0_attn_A_log, L0_attn_D, L0_attn_x_proj_w, L0_attn_dt_proj_w, L0_attn_dt_proj_b, L0_ffn_W_res, L0_ffn_W_pre, L0_ffn_W_post, L0_ffn_H_res_base, L0_ffn_H_pre_base, L0_ffn_H_post_base, L0_ffn_gate, L0_ffn_W_branch):

    def _L0_attn_ref(x, A_log, D, x_proj_w, dt_proj_w, dt_proj_b):
        import jax, jax.numpy as jnp
        import numpy as np
        import math
        D_MODEL = 1024
        D_STATE = 16
        EXPAND = 2
        D_INNER = D_MODEL * EXPAND
        DT_RANK = math.ceil(D_MODEL / 16)
        BATCH, SEQ_LEN = (2, 256)
        A = -jnp.exp(A_log)
        xp = jnp.einsum('bld,rd->blr', x, x_proj_w)
        dt_in = xp[..., :DT_RANK]
        B = xp[..., DT_RANK:DT_RANK + D_STATE]
        C = xp[..., DT_RANK + D_STATE:]
        dt = jax.nn.softplus(jnp.einsum('blr,dr->bld', dt_in, dt_proj_w) + dt_proj_b)
        dA = jnp.exp(dt[..., None] * A)
        dBx = dt[..., None] * B[:, :, None, :] * x[..., None]

        def step(h, inp):
            dA_t, dBx_t, C_t = inp
            h = dA_t * h + dBx_t
            y = jnp.einsum('bdn,bn->bd', h, C_t)
            return (h, y)
        h0 = jnp.zeros((x.shape[0], D_INNER, D_STATE), dtype=x.dtype)
        _, ys = jax.lax.scan(step, h0, (jnp.moveaxis(dA, 1, 0), jnp.moveaxis(dBx, 1, 0), jnp.moveaxis(C, 1, 0)))
        y = jnp.moveaxis(ys, 0, 1) + D * x
        return y

    def _L0_ffn_ref(x, W_res, W_pre, W_post, H_res_base, H_pre_base, H_post_base, gate, W_branch):
        import jax, jax.numpy as jnp
        import numpy as np
        N_STREAMS = 4
        DIM = 512
        SINKHORN_ITERS = 50
        SINKHORN_TAU = 0.1
        RMS_EPS = 1.1920929e-07

        def sinkhorn_log(logits, num_iters=SINKHORN_ITERS, tau=SINKHORN_TAU):
            Z = logits / tau
            u0 = jnp.zeros(Z.shape[:-1], Z.dtype)
            v0 = jnp.zeros_like(u0)

            def step(carry, _):
                u, v = carry
                u = -jax.nn.logsumexp(Z + v[..., None, :], axis=-1)
                v = -jax.nn.logsumexp(Z + u[..., :, None], axis=-2)
                return ((u, v), None)
            (u, v), _ = jax.lax.scan(step, (u0, v0), None, length=num_iters)
            return jnp.exp(Z + u[..., :, None] + v[..., None, :])
        B, T, nC = x.shape
        n = N_STREAMS
        C = nC // n
        x_norm = x * jax.lax.rsqrt(jnp.mean(x * x, axis=-1, keepdims=True) + RMS_EPS)
        H_res_logits = (x_norm @ W_res.T).reshape(B, T, n, n) + H_res_base
        H_pre_logits = x_norm @ W_pre.T + H_pre_base
        H_post_logits = x_norm @ W_post.T + H_post_base
        H_res = sinkhorn_log(H_res_logits)
        H_pre = jax.nn.softmax(H_pre_logits, axis=-1)
        H_post = jax.nn.softmax(H_post_logits, axis=-1)
        g = jax.nn.sigmoid(gate)[0]
        I = jnp.eye(n, dtype=H_res.dtype)
        H_res = (1.0 - g) * I + g * H_res
        x_streams = x.reshape(B, T, n, C)
        x_pre = jnp.einsum('btnc,btn->btc', x_streams, H_pre)
        y = x_pre @ W_branch
        x_mixed = jnp.einsum('btij,btjc->btic', H_res, x_streams)
        y_distributed = jnp.einsum('btc,btn->btnc', y, H_post)
        return (x_mixed + y_distributed).reshape(B, T, nC)
    x = L0_attn_x
    x = x + 0.5 * _L0_ffn_ref(_layernorm(x, axis=-1), L0_ffn_W_res, L0_ffn_W_pre, L0_ffn_W_post, L0_ffn_H_res_base, L0_ffn_H_pre_base, L0_ffn_H_post_base, L0_ffn_gate, L0_ffn_W_branch)
    x = x + _L0_attn_ref(_layernorm(x, axis=-1), L0_attn_A_log, L0_attn_D, L0_attn_x_proj_w, L0_attn_dt_proj_w, L0_attn_dt_proj_b)
    x = x + 0.5 * _L0_ffn_ref(_layernorm(x, axis=-1), L0_ffn_W_res, L0_ffn_W_pre, L0_ffn_W_post, L0_ffn_H_res_base, L0_ffn_H_pre_base, L0_ffn_H_post_base, L0_ffn_gate, L0_ffn_W_branch)
    return x

_drawn_inputs = setup_inputs


def setup_inputs(seed=0):
    import zlib

    import numpy as np

    out = dict(_drawn_inputs(seed))
    spreads = {'L0_attn_D': (1.0, 0.2), 'L0_ffn_H_post_base': (0.0, 0.8)}
    factors = {}
    for name, (base, spread) in spreads.items():
        noise = np.random.default_rng([zlib.crc32(name.encode()), seed]).standard_normal(out[name].shape)
        drawn = base * np.exp(spread * noise) if base else spread * noise
        out[name] = jnp.asarray(drawn.astype(out[name].dtype))
    for name, factor in factors.items():
        out[name] = (out[name] * factor).astype(out[name].dtype)
    return out
```

```python
from contextlib import ExitStack

import concourse.bass as bass
from concourse import mybir

F32 = mybir.dt.float32
ALU = mybir.AluOpType
ACT = mybir.ActivationFunctionType
AX = mybir.AxisListType

P = 128
BATCH, SEQ, D = 2, 2048, 2048
TOKENS = BATCH * SEQ
STREAMS = 4
W = D // STREAMS
KB = W // P
DT = D // P
TPR = P // STREAMS
Q = 4
GT = Q * TPR
G = 8
R = G * Q
BLOCKS = TOKENS // (G * GT)
S = 16
RANK = 64
NP = RANK + 2 * S
NL = 24
T = 512
CHUNKS = TOKENS // T
CPB = SEQ // T
LN_EPS = 1e-5
RMS_EPS = 1.1920929e-07
TAU_INV = 10.0
ITERS_PER_ABSORB = 7
ABSORBS = 7
ASKS = 6 + 2 * ABSORBS
STEPS = 17 + (6 * ITERS_PER_ABSORB - 1) * ABSORBS
ONE, TWO = 1, 2

C_IDENT = 0
C_SEL = C_IDENT + P
C_STREAM = C_SEL + Q * P
C_TOKEN = C_STREAM + STREAMS
C_HALF = C_TOKEN + TPR
C_COLS = C_HALF + 32


class Memory:

    def __init__(self, nc, ctx, tag):
        self.nc, self.ctx, self.tag = nc, ctx, tag

    def sb(self, name, shape):
        return self.ctx.enter_context(self.nc.sbuf_tensor(f"{self.tag}_{name}", shape, F32))

    def ps(self, name, shape):
        return self.ctx.enter_context(self.nc.psum_tensor(f"{self.tag}_{name}", shape, F32))


def signals(nc, ctx, tag, names, pairs=("stored",)):
    s = {n: ctx.enter_context(nc.semaphore(f"{tag}_{n}")) for n in names}
    for n in pairs:
        s[n] = [ctx.enter_context(nc.semaphore(f"{tag}_{n}{h}")) for h in range(2)]
    return s


class Chain:

    def __init__(self, eng, sem, base):
        self.eng, self.sem, self.base, self.steps = eng, sem, base, 0

    def done(self, ins):
        ins.then_inc(self.sem, 1)
        self.steps += 1

    def wait(self):
        self.eng.wait_ge(self.sem, self.base + self.steps)

    def then(self, ins):
        self.done(ins)
        self.wait()


def bcast(ap, shape):
    return ap.broadcast_to(shape)


def row_statistics(nc, e, m, s, rows, b, rms):
    V = nc.vector
    with e.Fori(0, R, 1) as r:
        e.wait_ge(s["loaded"], b * 16 + 16)
        V.bn_stats(m.bn[:, bass.ds(r, 1), :], rows[:, bass.ds((b % 2) * R + r, 1), :]).then_inc(s["bn"], 1)
    e.wait_ge(s["bn"], b * R + R)
    c = Chain(e, s["stat"], b * (26 if rms else 18))
    c.done(V.tensor_tensor(m.mvc[:, 0, :], m.bn[:, :, 1], m.bn[:, :, 4], ALU.add))
    c.done(V.tensor_tensor(m.dev[:, :], m.bn[:, :, 1], m.bn[:, :, 4], ALU.subtract))
    c.then(V.tensor_tensor(m.dev2[:, :], m.bn[:, :, 2], m.bn[:, :, 5], ALU.add))
    c.then(V.tensor_tensor(m.dev[:, :], m.dev[:, :], m.dev[:, :], ALU.mult))
    c.then(V.scalar_tensor_tensor(m.mvc[:, 1, :], m.dev[:, :], W / 4, m.dev2[:, :], ALU.mult, ALU.add))
    c.done(V.transpose(m.mT[:, 0, :], m.mvc[:, 0, :]))
    c.then(V.transpose(m.mT[:, 1, :], m.mvc[:, 1, :]))
    mT = m.mT[:, 0, :].rearrange("p (t j) -> p t j", j=STREAMS)
    vT = m.mT[:, 1, :].rearrange("p (t j) -> p t j", j=STREAMS)
    dT = m.dT[:, :].rearrange("p (t j) -> p t j", j=STREAMS)
    mean, rstd, ms, std = (m.tok[:, k, :] for k in range(4))
    c.then(V.tensor_reduce(m.sum8[:, :], mT, AX.X, ALU.add))
    c.done(V.tensor_scalar(mean, m.sum8[:, :], 1.0 / (2 * STREAMS), None, ALU.mult))
    c.then(V.tensor_scalar(m.t8[:, :], m.sum8[:, :], 1.0 / STREAMS, None, ALU.mult))
    c.then(V.tensor_tensor(dT, mT, bcast(m.t8[:, :].unsqueeze(2), [P, 8, STREAMS]), ALU.subtract))
    c.then(V.tensor_tensor(dT, dT, dT, ALU.mult))
    c.then(V.scalar_tensor_tensor(dT, dT, W / 4, vT, ALU.mult, ALU.add))
    c.then(V.tensor_reduce(m.var8[:, :], dT, AX.X, ALU.add))
    V.tensor_scalar(m.ve[:, :], m.var8[:, :], 1.0 / D, LN_EPS, ALU.mult, ALU.add).then_inc(s["ve"], 1)
    e.wait_ge(s["pow"], (b * 2 if rms else b) + 1)
    if rms:
        c.then(V.tensor_scalar(m.var8[:, :], m.var8[:, :], 1.0 / D, None, ALU.mult))
        c.then(V.tensor_tensor(m.t8[:, :], m.var8[:, :], m.pow1[:, :], ALU.mult))
        c.then(V.tensor_tensor(m.t8[:, :], m.t8[:, :], m.pow1[:, :], ALU.mult))
        V.tensor_scalar(m.msq[:, :], m.t8[:, :], RMS_EPS, None, ALU.add).then_inc(s["ve"], 1)
        e.wait_ge(s["pow"], b * 2 + 2)
        c.done(V.tensor_tensor(rstd, m.pow1[:, :], m.pow2[:, :], ALU.mult))
        c.then(V.tensor_tensor(ms, m.msq[:, :], m.pow2[:, :], ALU.mult))
        c.then(V.tensor_tensor(m.t8[:, :], m.ve[:, :], m.pow1[:, :], ALU.mult))
        c.then(V.tensor_tensor(std, m.t8[:, :], ms, ALU.mult))
    else:
        c.then(V.tensor_copy(rstd, m.pow1[:, :]))
    n = 4 if rms else 2
    c.then(V.tensor_copy(m.tokx[:, 0:8 * n, :], bcast(
        m.tok[:, 0:n, :].rearrange("p a t -> p (a t)").unsqueeze(2), [P, 8 * n, STREAMS])))
    for k in range(n):
        ins = V.transpose(m.rowt[:, k, :], m.tokx[:, 8 * k:8 * k + 8, :].rearrange("p t j -> p (t j)"))
        c.then(ins) if k == n - 1 else c.done(ins)
    V.tensor_copy(m.row[:, bass.ds((b % 2) * 4, n), :], m.rowt[:, 0:n, :]).then_inc(s["row"], 1)
    assert c.steps == (26 if rms else 18), c.steps
    with e.Fori(0, R, 1) as r:
        e.wait_ge(s["row"], b + 1)
        V.tensor_scalar(rows[:, bass.ds((b % 2) * R + r, 1), :], rows[:, bass.ds((b % 2) * R + r, 1), :],
                        m.row[:, bass.ds((b % 2) * 4, 1), bass.ds(r, 1)].rearrange("p a b -> p (a b)"),
                        m.row[:, bass.ds((b % 2) * 4 + 1, 1), bass.ds(r, 1)].rearrange("p a b -> p (a b)"),
                        ALU.subtract, ALU.mult).then_inc(s["norm"], 1)


def statistics_buffers(m):
    m.bn = m.sb("bn", [P, R, 6])
    m.dev = m.sb("dev", [P, R])
    m.dev2 = m.sb("dev2", [P, R])
    m.mvc = m.sb("mvc", [P, 2, R])
    m.mT = m.sb("mT", [P, 2, 32])
    m.dT = m.sb("dT", [P, 32])
    m.sum8, m.var8, m.ve, m.msq, m.pow1, m.pow2, m.t8 = (
        m.sb(n, [P, 8]) for n in ("sum8", "var8", "ve", "msq", "pow1", "pow2", "t8"))
    m.tok = m.sb("tok", [P, 4, 8])
    m.tokx = m.sb("tokx", [P, 32, STREAMS])
    m.rowt = m.sb("rowt", [P, 4, R])
    m.row = m.sb("row", [P, 8, R])


def pool_roots(nc, e, m, s, b, rms):
    e.wait_ge(s["ve"], (b * 2 if rms else b) + 1)
    nc.gpsimd.tensor_tensor(m.pow1[:, :], m.ve[:, :], m.minus_half, ALU.pow).then_inc(s["pow"], 1)
    if rms:
        e.wait_ge(s["ve"], b * 2 + 2)
        nc.gpsimd.tensor_tensor(m.pow2[:, :], m.msq[:, :], m.minus_half, ALU.pow).then_inc(s["pow"], 1)


def ffn_program(nc, tag, s, src, dst, consts, w_logit, base, gate, w_branch):
    with ExitStack() as ctx:
        m = Memory(nc, ctx, tag)
        V, A, PE, POOL = nc.vector, nc.scalar, nc.tensor, nc.gpsimd
        const = m.sb("const", [P, C_COLS])
        ident = const[:, C_IDENT:C_IDENT + P]
        sel = const[:, C_SEL:C_SEL + Q * P].rearrange("p (q n) -> p q n", q=Q)
        stream_mask = const[:, C_STREAM:C_STREAM + STREAMS]
        token_mask = const[:, C_TOKEN:C_TOKEN + TPR]
        m.minus_half = const[:, C_HALF:C_HALF + 8]
        statistics_buffers(m)
        xh = m.sb("xh", [P, 2 * R, W])
        wl = m.sb("wl", [P, DT, NL])
        wb = m.sb("wb", [P, KB, W])
        base_b = m.sb("base_b", [P, NL])
        gate_b, ge, gs, g_half, i_half = (
            m.sb(n, [P, 1]) for n in ("gate_b", "ge", "gs", "g_half", "i_half"))
        xT = m.sb("xT", [P, 2, DT, GT])
        lg = m.sb("lg", [P, G, NL])
        z, pr, tmp = (m.sb(n, [P, G, 16]) for n in ("z", "pr", "tmp"))
        uv, luv = (m.sb(n, [P, 2, G, 4]) for n in ("uv", "luv"))
        sm = m.sb("sm", [P, G, 4])
        hp = m.sb("hp", [P, 2 * G, 4])
        hpm = m.sb("hpm", [P, 2 * G])
        h5 = m.sb("h5", [P, G, 5, 4])
        h_post = m.sb("h_post", [P, G, 4])
        rep = m.sb("rep", [P, 2 * G * 5, 4])
        m5 = m.sb("m5", [P, Q, G, 5])
        dsc = m.sb("dsc", [P, R])
        dm = m.sb("dm", [P, Q, G, 4])
        mix_blk = m.sb("mix_blk", [P, 2, Q, TPR, 4])
        pre_blk = m.sb("pre_blk", [P, 2, Q, TPR])
        post_blk = m.sb("post_blk", [P, 2, Q * TPR, 4])
        xpT = m.sb("xpT", [P, KB * GT])
        y_sb = m.sb("y_sb", [P, W])
        o_sb = m.sb("o_sb", [P, 2, Q, W])
        tp = [m.ps(f"tp{i}", [P, W]) for i in range(2)]
        lp = m.ps("lp", [P, NL])
        rp = m.ps("rp", [P, 2 * G * 20])
        xp = m.ps("xp", [P, W])
        yp = m.ps("yp", [P, W])
        op = [m.ps(f"op{i}", [P, W]) for i in range(2)]
        block = ctx.enter_context(nc.Block())

        @block.sync
        def _(sp):
            sp.dma_start(const[:, :], consts).then_inc(s["const"], 16)
            sp.dma_start(wl[:, :, :], w_logit).then_inc(s["weights"], 16)
            sp.dma_start(wb[:, :, :], w_branch).then_inc(s["weights"], 16)
            sp.dma_start(base_b[:, :], base.partition_broadcast(P)).then_inc(s["weights"], 16)
            sp.dma_start(gate_b[:, :], gate.partition_broadcast(P)).then_inc(s["weights"], 16)
            for b in range(BLOCKS):
                if b >= 2:
                    sp.wait_ge(s["o_out"], TWO + (b - 1) * R)
                sp.dma_start(xh[:, (b % 2) * R:(b % 2 + 1) * R, :],
                             src[b * R * P:(b + 1) * R * P, :].rearrange("(r p) c -> p r c", p=P)
                             ).then_inc(s["loaded"], 16)
                sp.wait_ge(s["loaded"], 16 * (b + 1))

        def row_tile(r, b):
            return xh[:, (b % 2) * R + r, :]

        def row_channels(r, b, k):
            return xh[:, (b % 2) * R + r, k * P:(k + 1) * P]

        @block.gpsimd
        def _(pool):
            pool.wait_ge(s["const"], 16)

            def build(b):
                with pool.Fori(0, G // 2, 1) as gg:
                    for h in range(2):
                        g = gg * 2 + h
                        pool.wait_ge(s["coef"], b + 1)
                        pool.wait_ge(s["blk_free"], b * G + g + 1)
                        POOL.tensor_tensor(
                            pre_blk[:, h, :, :], bcast(token_mask.unsqueeze(1), [P, Q, TPR]),
                            bcast(m5[:, :, bass.ds(g, 1), 4], [P, Q, TPR]), ALU.mult).then_inc(s["pre_blk"], 1)
                        for q in range(Q):
                            POOL.tensor_tensor(
                                mix_blk[:, h, q, :, :], bcast(token_mask.unsqueeze(2), [P, TPR, 4]),
                                bcast(m5[:, q, bass.ds(g, 1), 0:4], [P, TPR, 4]),
                                ALU.mult).then_inc(s["mix_blk"], 1)
                        POOL.tensor_tensor(
                            post_blk[:, h, :, :], bcast(ident.unsqueeze(2), [P, P, 4]),
                            bcast(h_post[:, bass.ds(g, 1), :], [P, P, 4]), ALU.mult).then_inc(s["post_blk"], 1)

            pool_roots(nc, pool, m, s, 0, True)
            with pool.Fori(0, BLOCKS - 1, 1) as b:
                pool_roots(nc, pool, m, s, b + 1, True)
                build(b)
            build(BLOCKS - 1)


        @block.tensor
        def _(pe):
            pe.wait_ge(s["const"], 16)
            pe.wait_ge(s["weights"], 64)
            pe.sem_inc(s["logits"], TWO)
            pe.sem_inc(s["y_full"], ONE)
            pe.sem_inc(s["o_full"], ONE)

            def logits(b):
                for g in range(G):
                    n = b * G + g
                    pe.wait_ge(s["norm"], n * Q + Q)
                    for k in range(KB):
                        pe.wait_ge(s["xT_in"], n * KB + k + 1)
                        for q in range(Q):
                            mm = PE.transpose(tp[k % 2][:, q * P:(q + 1) * P],
                                              row_channels(g * Q + q, b, k), ident)
                        mm.then_inc(s["tp_full"], 1)
                    pe.wait_ge(s["xT_in"], TWO + n * KB + KB)
                    pe.wait_ge(s["lg_in"], n + 1)
                    for d in range(DT):
                        mm = PE.matmul(lp[:, :], xT[:, g % 2, d, :], wl[:, d, :],
                                       start=(d == 0), stop=(d == DT - 1))
                    mm.then_inc(s["logits"], 1)

            def coefficients_to_rows(b):
                pe.wait_ge(s["h5"], b + 1)
                for half in range(2):
                    pe.wait_ge(s["rp_free"], b * 2 + half + 1)
                    for q in range(2):
                        mm = PE.matmul(rp[:, q * G * 20:(q + 1) * G * 20], sel[:, half * 2 + q, :],
                                       h5[:, :, :, :].rearrange("p g i j -> p (g i j)"),
                                       start=True, stop=True)
                    mm.then_inc(s["rp_full"], 1)

            def mix(b):
                for g in range(G):
                    n, h = b * G + g, g % 2
                    pe.wait_ge(s["pre_blk"], n + 1)
                    pe.wait_ge(s["xpT_in"], n + 1)
                    for k in range(KB):
                        for q in range(Q):
                            mm = PE.matmul(xp[:, k * GT + q * TPR:k * GT + (q + 1) * TPR],
                                           row_channels(g * Q + q, b, k), pre_blk[:, h, q, :],
                                           start=True, stop=True)
                    mm.then_inc(s["xp_full"], 1)
                    pe.wait_ge(s["xpT_in"], ONE + n + 1)
                    pe.wait_ge(s["y_in"], n + 1)
                    for k in range(KB):
                        mm = PE.matmul(yp[:, :], xpT[:, k * GT:(k + 1) * GT], wb[:, k, :],
                                       start=(k == 0), stop=(k == KB - 1))
                    mm.then_inc(s["y_full"], 1)
                    pe.wait_ge(s["mix_blk"], n * Q + Q)
                    pe.wait_ge(s["post_blk"], ONE + n + 1)
                    pe.wait_ge(s["y_in"], ONE + n + 1)
                    for q in range(Q):
                        pe.wait_ge(s["o_out"], n * Q + q + 1)
                        PE.matmul(op[q % 2][:, :], mix_blk[:, h, q, :, :].rearrange("p t i -> p (t i)"),
                                  row_tile(g * Q + q, b), start=True, stop=False)
                        PE.matmul(op[q % 2][:, :], post_blk[:, h, q * TPR:(q + 1) * TPR, :]
                                  .rearrange("p t i -> p (t i)"), y_sb[:, :],
                                  start=False, stop=True).then_inc(s["o_full"], 1)

            logits(0)
            for b in range(BLOCKS):
                coefficients_to_rows(b)
                if b + 1 < BLOCKS:
                    logits(b + 1)
                mix(b)

        @block.scalar
        def _(act):
            act.wait_ge(s["weights"], 64)
            A.activation(ge[:, :], gate_b[:, :], ACT.Exp, scale=-1.0).then_inc(s["gate"], 1)
            act.sem_inc(s["xT_in"], TWO)
            act.sem_inc(s["xpT_in"], ONE)
            act.sem_inc(s["y_in"], ONE)
            act.sem_inc(s["o_out"], TWO)
            act.sem_inc(s["blk_free"], TWO)
            act.sem_inc(s["stored"][0], 16)
            act.sem_inc(s["stored"][1], 16)

            def transposed(b):
                with act.Fori(0, G // 2, 1) as gg:
                    for h in range(2):
                        n = b * G + gg * 2 + h
                        act.wait_ge(s["logits"], n + 1)
                        for k in range(KB):
                            act.wait_ge(s["tp_full"], n * KB + k + 1)
                            A.activation(xT[:, h, k::KB, :],
                                         tp[k % 2][:, :].rearrange("p (n j) -> p j n", j=STREAMS),
                                         ACT.Copy).then_inc(s["xT_in"], 1)

            def softmax_functions(b):
                for i, (out, in_, f) in enumerate(
                        [(hp[:, :, :], hp[:, :, :], ACT.Exp)]
                        + [(tmp[:, :, :], z[:, :, :], ACT.Exp), (sm[:, :, :], sm[:, :, :], ACT.Ln)] * 2
                        + [(pr[:, :, :], z[:, :, :], ACT.Exp)]):
                    act.wait_ge(s["ask"], b * ASKS + i + 1)
                    A.activation(out, in_, f).then_inc(s["given"], 1)

            def absorb_functions(b, a):
                act.wait_ge(s["ask"], b * ASKS + 6 + a * 2 + 1)
                A.activation(luv[:, :, :, :], uv[:, :, :, :], ACT.Ln).then_inc(s["given"], 1)
                act.wait_ge(s["ask"], b * ASKS + 6 + a * 2 + 2)
                A.activation(pr[:, :, :], z[:, :, :], ACT.Exp).then_inc(s["given"], 1)

            def mixed(b, g, h):
                n = b * G + g
                act.wait_ge(s["xp_full"], n + 1)
                act.wait_ge(s["y_full"], n + 1)
                A.activation(xpT[:, :], xp[:, :], ACT.Copy).then_inc(s["xpT_in"], 1)
                act.wait_ge(s["y_full"], ONE + n + 1)
                act.wait_ge(s["o_full"], n * Q + 1)
                A.activation(y_sb[:, :], yp[:, :], ACT.Copy).then_inc(s["y_in"], 1)
                act.wait_ge(s["stored"][h], (b * (G // 2) + (g - h) // 2 + 1) * 16)
                for q in range(Q):
                    act.wait_ge(s["o_full"], ONE + n * Q + q + 1)
                    A.activation(o_sb[:, h, q, :], op[q % 2][:, :], ACT.Identity,
                                 bias=m.row[:, bass.ds((b % 2) * 4, 1), bass.ds(g * Q + q, 1)]
                                 .rearrange("p a b -> p (a b)")).then_inc(s["o_out"], 1)
                act.sem_inc(s["blk_free"], 1)
                act.wait_ge(s["o_out"], TWO + n * Q + Q)
                act.dma_start(dst[bass.ts(n, Q * P), :].rearrange("(q p) c -> p q c", p=P),
                              o_sb[:, h, :, :]).then_inc(s["stored"][h], 16)

            transposed(0)
            softmax_functions(0)
            with act.Fori(0, ABSORBS, 1) as a:
                absorb_functions(0, a)
            with act.Fori(0, BLOCKS - 1, 1) as b:
                transposed(b + 1)
                mixed(b, 0, 0)
                softmax_functions(b + 1)
                for g in range(1, G):
                    mixed(b, g, g % 2)
                    absorb_functions(b + 1, g - 1)
            for g in range(G):
                mixed(BLOCKS - 1, g, g % 2)
            for h in range(2):
                act.wait_ge(s["stored"][h], 16 + 16 * BLOCKS * G // 2)

        @block.vector
        def _(dve):
            dve.wait_ge(s["weights"], 64)
            dve.wait_ge(s["const"], 16)
            dve.sem_inc(s["lg_in"], ONE)
            dve.sem_inc(s["rp_free"], ONE)
            dve.sem_inc(s["post_blk"], ONE)
            c0 = Chain(dve, s["setup"], 0)
            dve.wait_ge(s["gate"], 1)
            c0.then(V.tensor_scalar(gs[:, :], ge[:, :], 1.0, None, ALU.add))
            c0.then(V.reciprocal(ge[:, :], gs[:, :]))
            c0.then(V.tensor_scalar(g_half[:, :], ge[:, :], 0.5, None, ALU.mult))
            c0.then(V.tensor_scalar(i_half[:, :], ge[:, :], -0.5, 0.5, ALU.mult, ALU.add))
            g4 = [P, G, 4, 4]

            def by_row(t):
                return t[:, :, :].rearrange("p g (i j) -> p g i j", i=4)

            def by_col(t):
                return t[:, :, :].rearrange("p g (i j) -> p g j i", i=4)

            def over(v):
                return bcast(v.unsqueeze(3), g4)

            with dve.Fori(0, BLOCKS, 1) as b:
                row_statistics(nc, dve, m, s, xh, b, True)
                with dve.Fori(0, G, 1) as g:
                    dve.wait_ge(s["logits"], TWO + b * G + g + 1)
                    V.tensor_tensor(lg[:, bass.ds(g, 1), :], lp[:, :].unsqueeze(1),
                                    base_b[:, :].unsqueeze(1), ALU.add).then_inc(s["lg_in"], 1)
                dve.wait_ge(s["lg_in"], ONE + b * G + G)

                c = Chain(dve, s["sink"], b * STEPS)
                asked = 0

                def ask(ins):
                    nonlocal asked
                    ins.then_inc(s["ask"], 1)
                    asked += 1
                    dve.wait_ge(s["given"], b * ASKS + asked)

                pp = lg[:, :, 16:24].rearrange("p g (s n) -> p g s n", s=2)
                hv = hp[:, :, :].rearrange("p (g s) n -> p g s n", s=2)
                c.then(V.tensor_reduce(hpm[:, :], pp, AX.X, ALU.max))
                ask(V.tensor_tensor(hv, pp, bcast(hpm[:, :].rearrange("p (g s) -> p g s", s=2)
                                                  .unsqueeze(3), [P, G, 2, 4]), ALU.subtract))
                c.then(V.tensor_reduce(hpm[:, :], hp[:, :, :], AX.X, ALU.add))
                c.then(V.reciprocal(hpm[:, :], hpm[:, :]))
                c.then(V.tensor_tensor(hp[:, :, :], hp[:, :, :],
                                       bcast(hpm[:, :].unsqueeze(2), [P, 2 * G, 4]), ALU.mult))
                c.then(V.tensor_scalar(z[:, :, :], lg[:, :, 0:16], TAU_INV, None, ALU.mult))
                for view in (by_row, by_col):
                    c.then(V.tensor_reduce(sm[:, :, :], view(z), AX.X, ALU.max))
                    ask(V.tensor_tensor(view(z), view(z), over(sm[:, :, :]), ALU.subtract))
                    ask(V.tensor_reduce(sm[:, :, :], view(tmp), AX.X, ALU.add))
                    ins = V.tensor_tensor(view(z), view(z), over(sm[:, :, :]), ALU.subtract)
                    if view is by_row:
                        c.then(ins)
                ins.then_inc(s["ask"], 1)
                first = c.steps
                with dve.Fori(0, ABSORBS, 1) as a:
                    dve.wait_ge(s["given"], b * ASKS + 6 + a * 2)
                    ca = Chain(dve, s["sink"], b * STEPS + first + a * (6 * ITERS_PER_ABSORB - 1))
                    for i in range(ITERS_PER_ABSORB):
                        if i:
                            ca.then(V.tensor_tensor(by_row(tmp), by_row(pr),
                                                    bcast(uv[:, 1, :, :].unsqueeze(2), g4), ALU.mult))
                        ca.then(V.tensor_reduce(sm[:, :, :], by_row(tmp if i else pr), AX.X, ALU.add))
                        ca.then(V.reciprocal(uv[:, 0, :, :], sm[:, :, :]))
                        ca.then(V.tensor_tensor(by_row(tmp), by_row(pr), over(uv[:, 0, :, :]), ALU.mult))
                        ca.then(V.tensor_reduce(sm[:, :, :], by_col(tmp), AX.X, ALU.add))
                        ins = V.reciprocal(uv[:, 1, :, :], sm[:, :, :])
                        if i < ITERS_PER_ABSORB - 1:
                            ca.then(ins)
                    ins.then_inc(s["ask"], 1)
                    dve.wait_ge(s["given"], b * ASKS + 6 + a * 2 + 1)
                    ca.then(V.tensor_tensor(by_row(z), by_row(z), over(luv[:, 0, :, :]), ALU.add))
                    V.tensor_tensor(by_row(z), by_row(z), bcast(luv[:, 1, :, :].unsqueeze(2), g4),
                                    ALU.add).then_inc(s["ask"], 1)
                    assert ca.steps == 6 * ITERS_PER_ABSORB - 1, ca.steps
                c.steps += (6 * ITERS_PER_ABSORB - 1) * ABSORBS
                dve.wait_ge(s["given"], b * ASKS + ASKS)
                dve.wait_ge(s["post_blk"], b * G + 1)
                c.done(V.tensor_copy(h5[:, :, 4, :], hv[:, :, 0, :]))
                c.done(V.tensor_scalar(h_post[:, :, :], hv[:, :, 1, :], 0.5, None, ALU.mult))
                V.tensor_scalar(h5[:, :, 0:4, :].rearrange("p g i j -> p g (i j)"), pr[:, :, :],
                                g_half[:, 0:1], None, ALU.mult).then_inc(s["h5"], 1)
                for half in range(2):
                    dve.wait_ge(s["rp_full"], b * 2 + half + 1)
                    c.then(V.tensor_tensor(rep[:, :, :], rp[:, :].rearrange("p (n j) -> p n j", j=4),
                                           bcast(stream_mask.unsqueeze(1), [P, 2 * G * 5, 4]), ALU.mult))
                    dve.sem_inc(s["rp_free"], 1)
                    c.then(V.tensor_reduce(m5[:, 2 * half:2 * half + 2, :, :].rearrange("p q g i -> p (q g i)"),
                                           rep[:, :, :], AX.X, ALU.add))
                slot = (b % 2) * 4
                ms = m.row[:, bass.ds(slot + 2, 1), :].rearrange("p a r -> p (a r)")
                std = m.row[:, bass.ds(slot + 3, 1), :].rearrange("p a r -> p (a r)")
                c.then(V.tensor_tensor(m5[:, :, :, :], m5[:, :, :, :], bcast(
                    ms.rearrange("p (g q) -> p q g", q=Q).unsqueeze(3), [P, Q, G, 5]), ALU.mult))
                c.then(V.scalar_tensor_tensor(dsc[:, :], ms, i_half[:, 0:1], std, ALU.mult, ALU.add))
                c.then(V.tensor_tensor(dm[:, :, :, :],
                                       bcast(dsc[:, :].rearrange("p (g q) -> p q g", q=Q).unsqueeze(3), [P, Q, G, 4]),
                                       bcast(stream_mask.unsqueeze(1).unsqueeze(1), [P, Q, G, 4]), ALU.mult))
                V.tensor_tensor(m5[:, :, :, 0:4], m5[:, :, :, 0:4], dm[:, :, :, :], ALU.add).then_inc(s["coef"], 1)
                assert asked == 5 and c.steps == STEPS, (asked, c.steps)


FFN_SIGNALS = ["const", "weights", "loaded", "coef", "blk_free", "pre_blk", "mix_blk", "post_blk", "norm",
               "tp_full", "xT_in", "logits", "lg_in", "h5", "rp_free", "rp_full", "xp_full", "xpT_in",
               "y_full", "y_in", "o_full", "o_out", "gate", "ask", "given", "setup", "sink",
               "bn", "stat", "ve", "pow", "row"]


def project_program(nc, tag, s, src, normed, projected, consts, w_proj):
    with ExitStack() as ctx:
        m = Memory(nc, ctx, tag)
        V, A, PE = nc.vector, nc.scalar, nc.tensor
        const = m.sb("const", [P, C_COLS])
        ident = const[:, C_IDENT:C_IDENT + P]
        m.minus_half = const[:, C_HALF:C_HALF + 8]
        statistics_buffers(m)
        xh = m.sb("xh", [P, 2 * R, W])
        wp = m.sb("wp", [P, DT, NP])
        CG = T // GT
        xT = m.sb("xT", [P, DT, 2, T])
        proj = m.sb("proj", [NP, T])
        tp = [m.ps(f"tp{i}", [P, W]) for i in range(4)]
        pp = [m.ps(f"pp{i}", [NP, T]) for i in range(2)]
        block = ctx.enter_context(nc.Block())
        FOUR = len(tp)

        @block.sync
        def _(sp):
            sp.dma_start(const[:, :], consts).then_inc(s["const"], 16)
            sp.dma_start(wp[:, :, :], w_proj).then_inc(s["weights"], 16)
            for b in range(BLOCKS):
                if b >= 2:
                    sp.wait_ge(s["tp_full"], (b - 1) * G * KB)
                sp.dma_start(xh[:, (b % 2) * R:(b % 2 + 1) * R, :],
                             src[b * R * P:(b + 1) * R * P, :].rearrange("(r p) c -> p r c", p=P)
                             ).then_inc(s["loaded"], 16)
                sp.wait_ge(s["loaded"], 16 * (b + 1))

        @block.gpsimd
        def _(pool):
            pool.wait_ge(s["const"], 16)
            for b in range(BLOCKS):
                pool_roots(nc, pool, m, s, b, False)

        @block.vector
        def _(dve):
            dve.wait_ge(s["const"], 16)
            with dve.Fori(0, BLOCKS, 1) as b:
                row_statistics(nc, dve, m, s, xh, b, False)


        @block.tensor
        def _(pe):
            pe.wait_ge(s["const"], 16)
            pe.wait_ge(s["weights"], 16)
            for b in range(BLOCKS):
                for g in range(G):
                    n = b * G + g
                    pe.wait_ge(s["norm"], n * Q + Q)
                    for k in range(KB):
                        pe.wait_ge(s["xT_in"], n * KB + k + 1)
                        for q in range(Q):
                            mm = PE.transpose(tp[k][:, q * P:(q + 1) * P],
                                              xh[:, (b % 2) * R + g * Q + q, k * P:(k + 1) * P], ident)
                        mm.then_inc(s["tp_full"], 1)
                    if g % CG == CG - 1:
                        c = n // CG
                        pe.wait_ge(s["xT_in"], FOUR + (n + 1) * KB)
                        pe.wait_ge(s["proj_in"], c + 1)
                        for d in range(DT):
                            mm = PE.matmul(pp[c % 2][:, :], wp[:, d, :], xT[:, d, c % 2, :],
                                           start=(d == 0), stop=(d == DT - 1))
                        mm.then_inc(s["proj_full"], 1)

        @block.scalar
        def _(act):
            act.sem_inc(s["xT_in"], FOUR)
            act.sem_inc(s["proj_in"], TWO)
            act.sem_inc(s["stored"][0], 16)
            act.sem_inc(s["stored"][0], 16)
            act.sem_inc(s["stored"][1], 16)
            with act.Fori(0, CHUNKS // 2, 1) as cc:
                for h in range(2):
                    c = cc * 2 + h
                    for g in range(CG):
                        n = c * CG + g
                        for k in range(KB):
                            act.wait_ge(s["tp_full"], n * KB + k + 1)
                            if g == 0 and k == 0:
                                act.wait_ge(s["stored"][0], (c + 1) * 16)
                                act.wait_ge(s["proj_in"], c + 1)
                            A.activation(xT[:, k::KB, h, g * GT:(g + 1) * GT],
                                         tp[k][:, :].rearrange("p (n j) -> p j n", j=STREAMS),
                                         ACT.Copy).then_inc(s["xT_in"], 1)
                    act.wait_ge(s["xT_in"], FOUR + (c + 1) * CG * KB)
                    act.dma_start(normed[bass.ts(c, DT * P), :].rearrange("(d p) t -> p d t", p=P),
                                  xT[:, :, h, :]).then_inc(s["stored"][0], 16)
                    act.wait_ge(s["proj_full"], c + 1)
                    act.wait_ge(s["stored"][1], (c + 1) * 16)
                    A.activation(proj[:, :], pp[h][:, :], ACT.Copy).then_inc(s["proj_in"], 1)
                    act.wait_ge(s["proj_in"], TWO + c + 1)
                    act.dma_start(projected[:, bass.ts(c, T)], proj[:, :]).then_inc(s["stored"][1], 16)
            act.wait_ge(s["stored"][0], 32 + 16 * CHUNKS)
            act.wait_ge(s["stored"][1], 16 + 16 * CHUNKS)


PROJECT_SIGNALS = ["const", "weights", "loaded", "norm", "tp_full", "xT_in", "proj_full", "proj_in",
                   "bn", "stat", "ve", "pow", "row"]

C_CHAN = S + 2
HSLOTS = 8
GSLOTS = 4
ASLOTS = 3
K = CHUNKS * DT


def scan_program(nc, tag, s, x_in, normed, projected, x_out, consts, channels, w_dt, keep):
    with ExitStack() as ctx:
        m = Memory(nc, ctx, tag)
        V, A, PE, POOL = nc.vector, nc.scalar, nc.tensor, nc.gpsimd
        ident = m.sb("ident", [P, P])
        keep_sb = m.sb("keep", [P, K])
        bc = m.sb("bc", [P, 2, 2 * S, T])
        dt_in = m.sb("dt_in", [RANK, 2, T])
        xn = m.sb("xn", [P, 2, T])
        x_blk = m.sb("x_blk", [P, 2, T // P, P])
        chan = m.sb("chan", [P, 2, C_CHAN])
        wdt = m.sb("wdt", [RANK, 2, P])
        neg_a = m.sb("neg_a", [P, 2, S])
        mag, ex, rl, ln1p = (m.sb(n, [P, T]) for n in ("mag", "ex", "rl", "ln1p"))
        neg_dt = m.sb("neg_dt", [P, 2, T])
        diag_d = m.sb("diag_d", [P, 2, P])
        h_last = m.sb("h_last", [P, DT, S])
        h_first = m.sb("h_first", [P, 2, S])
        bx = m.sb("bx", [P, ASLOTS, T])
        hs = m.sb("hs", [P, HSLOTS, T])
        ch = m.sb("ch", [P, GSLOTS, T])
        y_sb = m.sb("y_sb", [P, T])
        o_sb = m.sb("o_sb", [P, 2, T // P, P])
        decay = [m.ps(f"decay{i}", [P, T]) for i in range(ASLOTS)]
        u = m.ps("u", [P, T])
        acc = [m.ps(f"acc{i}", [P, T]) for i in range(2)]
        dt_raw = m.ps("dt_raw", [P, T])
        turned = m.ps("turned", [P, T])
        block = ctx.enter_context(nc.Block())
        x_tok = x_in.rearrange("(n j) c -> n (j c)", j=STREAMS)
        out_tok = x_out.rearrange("(n j) c -> n (j c)", j=STREAMS)

        def token_block(x, k):
            return x[bass.ds((k // DT) * T, T), bass.ds((k % DT) * P, P)].rearrange("(a p) c -> p a c", p=P)

        def reuse(n):
            return ASLOTS if n == 0 else 1


        @block.sync
        def _(sp):
            def load(k, h):
                sp.wait_ge(s["turned"], k + 1)
                sp.dma_start(xn[:, h, :], normed[bass.ts(k, P), :]).then_inc(s["loaded"][h], 16)
                sp.dma_start(chan[:, h, :], channels[bass.ts(k % DT, P), :]).then_inc(s["loaded"][h], 16)
                sp.dma_start(wdt[:, h, :], w_dt[bass.ts(k % DT, RANK), :]).then_inc(s["loaded"][h], 16)
                sp.dma_start(x_blk[:, h, :, :], token_block(x_tok, k)).then_inc(s["loaded"][h], 16)

            def load_chunk(c):
                sp.dma_start(dt_in[:, bass.ds(c % 2, 1), :],
                             projected[0:RANK, bass.ts(c, T)].unsqueeze(1)).then_inc(s["chunk"], 16)
                sp.dma_start(bc[:, bass.ds(c % 2, 1), :, :],
                             projected[RANK:NP, bass.ts(c, T)].unsqueeze(0).partition_broadcast(P)
                             ).then_inc(s["chunk"], 16)

            sp.dma_start(ident[:, :], consts[:, C_IDENT:C_IDENT + P]).then_inc(s["const"], 16)
            sp.dma_start(keep_sb[:, :], keep).then_inc(s["const"], 16)
            load_chunk(0)
            with sp.Fori(0, CHUNKS - 1, 1) as c:
                for h in range(2):
                    load(c * DT + h, h)
                sp.wait_ge(s["chunk"], c * 32 + 32)
                sp.wait_ge(s["scaled"], HSLOTS + c * DT * S)
                load_chunk(c + 1)
                with sp.Fori(1, DT // 2, 1) as i:
                    for h in range(2):
                        load(c * DT + i * 2 + h, h)
            with sp.Fori(0, DT // 2, 1) as i:
                for h in range(2):
                    load((CHUNKS - 1) * DT + i * 2 + h, h)

        @block.scalar
        def _(act):
            act.sem_inc(s["dt_read"], ONE)
            act.sem_inc(s["y_in"], ONE)
            act.sem_inc(s["turned_in"], ONE)
            act.sem_inc(s["stored"][0], 16)
            act.sem_inc(s["stored"][1], 16)

            def step(k, h, first=False):
                act.wait_ge(s["loaded"][h], (k // 2) * 64 + 64)
                A.activation(neg_a[:, h, :], chan[:, h, 0:S], ACT.Exp).then_inc(s["neg_a"], 1)
                act.wait_ge(s["dt_raw"], k + 1)
                A.activation(mag[:, :], dt_raw[:, :], ACT.Abs, bias=chan[:, h, S + 1:S + 2]).then_inc(s["soft"], 1)
                act.wait_ge(s["neg_dt"], k + 1)
                A.activation(rl[:, :], dt_raw[:, :], ACT.Relu, bias=chan[:, h, S + 1:S + 2]).then_inc(s["dt_read"], 1)
                act.wait_ge(s["soft"], k * 3 + 1)
                A.activation(ex[:, :], mag[:, :], ACT.Exp, scale=-1.0).then_inc(s["soft"], 1)
                act.wait_ge(s["soft"], k * 3 + 2)
                A.activation(ln1p[:, :], ex[:, :], ACT.Ln, bias=1.0).then_inc(s["soft"], 1)
                act.wait_ge(s["soft"], k * 3 + 3)
                act.wait_ge(s["neg_a"], k + 1)
                for n in range(S):
                    U = k * S + n
                    if n == 0:
                        act.wait_ge(s["neg_dt"], ONE + k + 1)
                    act.wait_ge(s["scan"], U + reuse(n))
                    A.activation(decay[n % ASLOTS][:, :], neg_dt[:, h, :], ACT.Exp,
                                 scale=neg_a[:, h, n:n + 1]).then_inc(s["decay"], 1)
                    if n == 6 and not first:
                        copy_sum(k - 1, 1 - h)
                    if n == 11 and not first:
                        copy_turned(k - 1, 1 - h)

            def copy_sum(k, h):
                act.wait_ge(s["summed"], GSLOTS + (k + 1) * S)
                act.wait_ge(s["turned"], TWO + k)
                A.activation(y_sb[:, :], acc[h][:, :], ACT.Copy).then_inc(s["y_in"], 1)

            def copy_turned(k, h):
                act.wait_ge(s["turned"], TWO + k + 1)
                act.wait_ge(s["stored"][h], (k // 2) * 16 + 16)
                A.activation(o_sb[:, h, :, :].rearrange("p a c -> p (a c)"), turned[:, :],
                             ACT.Copy).then_inc(s["turned_in"], 1)
                act.wait_ge(s["turned_in"], ONE + k + 1)
                act.dma_start(token_block(out_tok, k), o_sb[:, h, :, :]).then_inc(s["stored"][h], 16)

            step(0, 0, True)
            with act.Fori(0, (K - 2) // 2, 1) as i:
                step(i * 2 + 1, 1)
                step(i * 2 + 2, 0)
            step(K - 1, 1)
            copy_sum(K - 1, 1)
            copy_turned(K - 1, 1)
            for h in range(2):
                act.wait_ge(s["stored"][h], 16 + 16 * K // 2)

        @block.vector
        def _(dve):
            dve.memset(h_last[:, :, :], 0.0).then_inc(s["state"], 1)
            dve.sem_inc(s["scan"], ASLOTS)
            dve.sem_inc(s["neg_dt"], ONE)
            dve.sem_inc(s["bx"], ONE)
            dve.wait_ge(s["const"], 32)

            def step(k, h):
                dve.wait_ge(s["loaded"][h], (k // 2) * 64 + 64)
                dve.wait_ge(s["state"], k * 2 + 1)
                V.tensor_scalar(h_first[:, h, :], h_last[:, bass.ds(k % DT, 1), :].rearrange("p a n -> p (a n)"),
                                keep_sb[:, bass.ds(k, 1)], None, ALU.mult).then_inc(s["first"], 1)
                V.tensor_scalar(diag_d[:, h, :], ident[:, :], chan[:, h, S:S + 1], None,
                                ALU.mult).then_inc(s["diag"], 1)
                dve.wait_ge(s["soft"], k * 3 + 3)
                dve.wait_ge(s["dt_read"], ONE + k + 1)
                V.scalar_tensor_tensor(neg_dt[:, h, :], rl[:, :], -1.0, ln1p[:, :],
                                       ALU.mult, ALU.subtract).then_inc(s["neg_dt"], 1)
                dve.wait_ge(s["neg_dt"], ONE + k + 1)
                dve.wait_ge(s["bx"], ONE + k * S)
                V.scalar_tensor_tensor(u[:, :], neg_dt[:, h, :], -1.0, xn[:, h, :],
                                       ALU.mult, ALU.mult).then_inc(s["u"], 1)
                dve.wait_ge(s["chunk"], (k // DT) * 32 + 32)
                dve.wait_ge(s["u"], k + 1)
                slot = (k // DT) % 2

                def make_input(n):
                    U = k * S + n
                    dve.wait_ge(s["scan"], U + reuse(n))
                    V.tensor_tensor(bx[:, n % ASLOTS, :], u[:, :], bc[:, bass.ds(slot, 1), n, :]
                                    .rearrange("p a t -> p (a t)"), ALU.mult).then_inc(s["bx"], 1)

                def scan(n):
                    U = k * S + n
                    if n == HSLOTS:
                        dve.wait_ge(s["state"], k * 2 + 2)
                    if n == 0:
                        dve.wait_ge(s["first"], k + 1)
                    dve.wait_ge(s["scaled"], U + 1)
                    dve.wait_ge(s["decay"], U + 1)
                    dve.wait_ge(s["bx"], ONE + U + 1)
                    V.tensor_tensor_scan(hs[:, n % HSLOTS, :], decay[n % ASLOTS][:, :], bx[:, n % ASLOTS, :],
                                         h_first[:, h, n:n + 1], ALU.mult, ALU.add).then_inc(s["scan"], 1)

                def save(half):
                    dve.wait_ge(s["scan"], ASLOTS + k * S + (half + 1) * HSLOTS)
                    V.tensor_scalar(h_last[:, bass.ds(k % DT, 1), half * HSLOTS:(half + 1) * HSLOTS],
                                    hs[:, :, T - 1].unsqueeze(1), 1.0, None, ALU.mult).then_inc(s["state"], 1)

                make_input(0)
                for n in range(S):
                    if n + 1 < S:
                        make_input(n + 1)
                    if n == HSLOTS:
                        save(0)
                    scan(n)
                save(1)

            with dve.Fori(0, K // 2, 1) as i:
                for h in range(2):
                    step(i * 2 + h, h)

        @block.gpsimd
        def _(pool):
            pool.sem_inc(s["scaled"], HSLOTS)
            with pool.Fori(0, K // 2, 1) as i:
                for h in range(2):
                    k = i * 2 + h
                    for n in range(S):
                        U = k * S + n
                        pool.wait_ge(s["summed"], U + 1)
                        pool.wait_ge(s["scan"], ASLOTS + U + 1)
                        POOL.tensor_tensor(ch[:, n % GSLOTS, :], hs[:, n % HSLOTS, :],
                                           bc[:, bass.ds((k // DT) % 2, 1), S + n, :]
                                           .rearrange("p a t -> p (a t)"), ALU.mult).then_inc(s["scaled"], 1)

        @block.tensor
        def _(pe):
            pe.sem_inc(s["summed"], GSLOTS)
            pe.sem_inc(s["turned"], TWO)
            pe.wait_ge(s["const"], 32)

            def raw_dt(k, h):
                pe.wait_ge(s["loaded"][h], (k // 2) * 64 + 64)
                pe.wait_ge(s["chunk"], (k // DT) * 32 + 32)
                pe.wait_ge(s["dt_read"], k + 1)
                PE.matmul(dt_raw[:, :], wdt[:, h, :], dt_in[:, bass.ds((k // DT) % 2, 1), :]
                          .rearrange("p a t -> p (a t)"), start=True, stop=True).then_inc(s["dt_raw"], 1)

            def turn(k, h):
                pe.wait_ge(s["turned_in"], k + 1)
                pe.wait_ge(s["y_in"], ONE + k + 1)
                PE.matmul(turned[:, :], ident[:, :], x_blk[:, h, :, :].rearrange("p a c -> p (a c)"),
                          start=True, stop=False)
                for a in range(T // P):
                    mm = PE.matmul(turned[:, a * P:(a + 1) * P], y_sb[:, a * P:(a + 1) * P], ident[:, :],
                                   start=False, stop=(a == T // P - 1))
                mm.then_inc(s["turned"], 1)

            def step(k, h, first=False, last=False):
                pe.wait_ge(s["diag"], k + 1)
                if not first:
                    pe.wait_ge(s["y_in"], k)
                PE.matmul(acc[h][:, :], diag_d[:, h, :], xn[:, h, :], start=True, stop=False)
                for n in range(S):
                    pe.wait_ge(s["scaled"], HSLOTS + k * S + n + 1)
                    mm = PE.matmul(acc[h][:, :], ident[:, :], ch[:, n % GSLOTS, :],
                                   start=False, stop=(n == S - 1))
                    mm.then_inc(s["summed"], 1)
                    if n == 10 and not last:
                        raw_dt(k + 1, 1 - h)
                    if n == 4 and not first:
                        turn(k - 1, 1 - h)

            raw_dt(0, 0)
            step(0, 0, first=True)
            with pe.Fori(0, (K - 2) // 2, 1) as i:
                step(i * 2 + 1, 1)
                step(i * 2 + 2, 0)
            step(K - 1, 1, last=True)
            turn(K - 1, 1)


SCAN_SIGNALS = ["const", "chunk", "turned", "dt_read", "y_in", "turned_in", "neg_a", "dt_raw", "soft",
                "neg_dt", "scan", "decay", "state", "first", "diag", "bx", "u", "scaled", "summed"]


def build(nc, x, w_logit, base, gate, w_branch, w_proj, channels, w_dt, consts, keep, out):
    def scratch(name, shape):
        return nc.dram_tensor(name, shape, F32, kind="Internal").ap()

    x1, x2 = (scratch(n, [TOKENS * STREAMS, W]) for n in ("x1", "x2"))
    normed = scratch("normed", [K * P, T])
    projected = scratch("projected", [NP, TOKENS])
    with ExitStack() as ctx:
        ffn1, ffn2 = (signals(nc, ctx, n, FFN_SIGNALS) for n in ("ffn1", "ffn2"))
        project = signals(nc, ctx, "project", PROJECT_SIGNALS)
        scan = signals(nc, ctx, "scan", SCAN_SIGNALS, ("stored", "loaded"))
        ffn_program(nc, "ffn1", ffn1, x, x1, consts, w_logit, base, gate, w_branch)
        project_program(nc, "project", project, x1, normed, projected, consts, w_proj)
        scan_program(nc, "scan", scan, x1, normed, projected, x2, consts, channels, w_dt, keep)
        ffn_program(nc, "ffn2", ffn2, x2, out, consts, w_logit, base, gate, w_branch)


def constants():
    import numpy as np
    p = np.arange(P)
    c = np.zeros((P, C_COLS), np.float32)
    c[:, C_IDENT:C_IDENT + P] = p[:, None] == p[None, :]
    for q in range(Q):
        c[:, C_SEL + q * P:C_SEL + (q + 1) * P] = p[:, None] == q * TPR + p[None, :] // STREAMS
    c[:, C_STREAM:C_STREAM + STREAMS] = p[:, None] % STREAMS == np.arange(STREAMS)
    c[:, C_TOKEN:C_TOKEN + TPR] = p[:, None] // STREAMS == np.arange(TPR)
    c[:, C_HALF:] = -0.5
    keep = np.ones((P, K), np.float32)
    keep[:, np.arange(K) // DT % CPB == 0] = 0.0
    return c, keep


def kernel(L0_attn_x, L0_attn_A_log, L0_attn_D, L0_attn_x_proj_w, L0_attn_dt_proj_w, L0_attn_dt_proj_b,
           L0_ffn_W_res, L0_ffn_W_pre, L0_ffn_W_post, L0_ffn_H_res_base, L0_ffn_H_pre_base,
           L0_ffn_H_post_base, L0_ffn_gate, L0_ffn_W_branch):
    import numpy as np
    import concourse.bacc as bacc
    from concourse.bass_utils import run_bass_kernel_spmd

    def tiles(w):
        return np.ascontiguousarray(w.T.reshape(-1, P, w.shape[0]).transpose(1, 0, 2))

    consts, keep = constants()
    arrays = {
        "x": np.ascontiguousarray(L0_attn_x).reshape(TOKENS * STREAMS, W),
        "w_logit": tiles(np.concatenate([L0_ffn_W_res, L0_ffn_W_pre, L0_ffn_W_post])),
        "base": np.concatenate([np.asarray(L0_ffn_H_res_base).reshape(-1), L0_ffn_H_pre_base, L0_ffn_H_post_base]),
        "gate": np.ascontiguousarray(L0_ffn_gate),
        "w_branch": np.ascontiguousarray(np.asarray(L0_ffn_W_branch).reshape(KB, P, W).transpose(1, 0, 2)),
        "w_proj": tiles(np.asarray(L0_attn_x_proj_w)),
        "channels": np.concatenate([L0_attn_A_log, np.asarray(L0_attn_D)[:, None],
                                    np.asarray(L0_attn_dt_proj_b)[:, None]], axis=1),
        "w_dt": np.ascontiguousarray(np.asarray(L0_attn_dt_proj_w).reshape(DT, P, RANK)
                                     .transpose(0, 2, 1)).reshape(DT * RANK, P),
        "consts": consts,
        "keep": keep,
    }
    nc = bacc.Bacc("TRN2", target_bir_lowering=False, num_devices=1)
    aps = {n: nc.dram_tensor(f"{n}_dram", a.shape, F32, kind="ExternalInput").ap() for n, a in arrays.items()}
    out = nc.dram_tensor("out_dram", [TOKENS * STREAMS, W], F32, kind="ExternalOutput").ap()
    build(nc, **aps, out=out)
    r = run_bass_kernel_spmd(nc, [{f"{n}_dram": a for n, a in arrays.items()}], core_ids=[0])
    return r.results[0]["out_dram"].reshape(BATCH, SEQ, D)
```

```python
from contextlib import ExitStack

import concourse.bass as bass
from concourse import mybir

F32 = mybir.dt.float32
ALU = mybir.AluOpType
ACT = mybir.ActivationFunctionType
AX = mybir.AxisListType

P = 128
BATCH, SEQ, D = 2, 2048, 2048
TOKENS = BATCH * SEQ
STREAMS = 4
W = D // STREAMS
KB = W // P
DT = D // P
TPR = P // STREAMS
Q = 4
GT = Q * TPR
G = 8
R = G * Q
BLOCKS = TOKENS // (G * GT)
S = 16
RANK = 64
NP = RANK + 2 * S
NL = 24
T = 512
CHUNKS = TOKENS // T
CPB = SEQ // T
LN_EPS = 1e-5
RMS_EPS = 1.1920929e-07
TAU_INV = 10.0
ITERS_PER_ABSORB = 7
ABSORBS = 7
ASKS = 6 + 2 * ABSORBS
STEPS = 17 + (6 * ITERS_PER_ABSORB - 1) * ABSORBS
EXP_AND_LN = "natural_log_exp_and_others"
ONE, TWO = 1, 2

C_IDENT = 0
C_SEL = C_IDENT + P
C_STREAM = C_SEL + Q * P
C_TOKEN = C_STREAM + STREAMS
C_HALF = C_TOKEN + TPR
C_COLS = C_HALF + 32


class Memory:

    def __init__(self, nc, ctx, tag):
        self.nc, self.ctx, self.tag = nc, ctx, tag

    def sb(self, name, shape):
        return self.ctx.enter_context(self.nc.sbuf_tensor(f"{self.tag}_{name}", shape, F32))

    def ps(self, name, shape):
        return self.ctx.enter_context(self.nc.psum_tensor(f"{self.tag}_{name}", shape, F32))


def signals(nc, ctx, tag, names, pairs=("stored",)):
    s = {n: ctx.enter_context(nc.semaphore(f"{tag}_{n}")) for n in names}
    for n in pairs:
        s[n] = [ctx.enter_context(nc.semaphore(f"{tag}_{n}{h}")) for h in range(2)]
    return s


class Chain:

    def __init__(self, eng, sem, base):
        self.eng, self.sem, self.base, self.steps = eng, sem, base, 0

    def done(self, ins):
        ins.then_inc(self.sem, 1)
        self.steps += 1

    def wait(self):
        self.eng.wait_ge(self.sem, self.base + self.steps)

    def then(self, ins):
        self.done(ins)
        self.wait()


def bcast(ap, shape):
    return ap.broadcast_to(shape)


def row_statistics(nc, e, m, s, rows, b, rms):
    V = nc.vector
    with e.Fori(0, G // 2, 1) as gg:
        for h in range(2):
            e.wait_ge(s["loaded"][h], 16 + (b * (G // 2) + gg + 1) * 16)
            for q in range(Q):
                r = (gg * 2 + h) * Q + q
                V.bn_stats(m.bn[:, bass.ds(r, 1), :], rows[:, bass.ds((b % 2) * R + r, 1), :]).then_inc(s["bn"], 1)
    e.wait_ge(s["bn"], b * R + R)
    c = Chain(e, s["stat"], b * (26 if rms else 18))
    c.done(V.tensor_tensor(m.mvc[:, 0, :], m.bn[:, :, 1], m.bn[:, :, 4], ALU.add))
    c.done(V.tensor_tensor(m.dev[:, :], m.bn[:, :, 1], m.bn[:, :, 4], ALU.subtract))
    c.then(V.tensor_tensor(m.dev2[:, :], m.bn[:, :, 2], m.bn[:, :, 5], ALU.add))
    c.then(V.tensor_tensor(m.dev[:, :], m.dev[:, :], m.dev[:, :], ALU.mult))
    c.then(V.scalar_tensor_tensor(m.mvc[:, 1, :], m.dev[:, :], W / 4, m.dev2[:, :], ALU.mult, ALU.add))
    c.done(V.transpose(m.mT[:, 0, :], m.mvc[:, 0, :]))
    c.then(V.transpose(m.mT[:, 1, :], m.mvc[:, 1, :]))
    mT = m.mT[:, 0, :].rearrange("p (t j) -> p t j", j=STREAMS)
    vT = m.mT[:, 1, :].rearrange("p (t j) -> p t j", j=STREAMS)
    dT = m.dT[:, :].rearrange("p (t j) -> p t j", j=STREAMS)
    mean, rstd, ms, std = (m.tok[:, k, :] for k in range(4))
    c.then(V.tensor_reduce(m.sum8[:, :], mT, AX.X, ALU.add))
    c.done(V.tensor_scalar(mean, m.sum8[:, :], 1.0 / (2 * STREAMS), None, ALU.mult))
    c.then(V.tensor_scalar(m.t8[:, :], m.sum8[:, :], 1.0 / STREAMS, None, ALU.mult))
    c.then(V.tensor_tensor(dT, mT, bcast(m.t8[:, :].unsqueeze(2), [P, 8, STREAMS]), ALU.subtract))
    c.then(V.tensor_tensor(dT, dT, dT, ALU.mult))
    c.then(V.scalar_tensor_tensor(dT, dT, W / 4, vT, ALU.mult, ALU.add))
    c.then(V.tensor_reduce(m.var8[:, :], dT, AX.X, ALU.add))
    V.tensor_scalar(m.ve[:, :], m.var8[:, :], 1.0 / D, LN_EPS, ALU.mult, ALU.add).then_inc(s["ve"], 1)
    e.wait_ge(s["pow"], (b * 2 if rms else b) + 1)
    if rms:
        c.then(V.tensor_scalar(m.var8[:, :], m.var8[:, :], 1.0 / D, None, ALU.mult))
        c.then(V.tensor_tensor(m.t8[:, :], m.var8[:, :], m.pow1[:, :], ALU.mult))
        c.then(V.tensor_tensor(m.t8[:, :], m.t8[:, :], m.pow1[:, :], ALU.mult))
        V.tensor_scalar(m.msq[:, :], m.t8[:, :], RMS_EPS, None, ALU.add).then_inc(s["ve"], 1)
        e.wait_ge(s["pow"], b * 2 + 2)
        c.done(V.tensor_tensor(rstd, m.pow1[:, :], m.pow2[:, :], ALU.mult))
        c.then(V.tensor_tensor(ms, m.msq[:, :], m.pow2[:, :], ALU.mult))
        c.then(V.tensor_tensor(m.t8[:, :], m.ve[:, :], m.pow1[:, :], ALU.mult))
        c.then(V.tensor_tensor(std, m.t8[:, :], ms, ALU.mult))
    else:
        c.then(V.tensor_copy(rstd, m.pow1[:, :]))
    n = 4 if rms else 2
    c.then(V.tensor_copy(m.tokx[:, 0:8 * n, :], bcast(
        m.tok[:, 0:n, :].rearrange("p a t -> p (a t)").unsqueeze(2), [P, 8 * n, STREAMS])))
    for k in range(n):
        ins = V.transpose(m.rowt[:, k, :], m.tokx[:, 8 * k:8 * k + 8, :].rearrange("p t j -> p (t j)"))
        c.then(ins) if k == n - 1 else c.done(ins)
    V.tensor_copy(m.row[:, bass.ds((b % 2) * 4, n), :], m.rowt[:, 0:n, :]).then_inc(s["row"], 1)
    assert c.steps == (26 if rms else 18), c.steps
    with e.Fori(0, G // 2, 1) as gg:
        e.wait_ge(s["row"], b + 1)
        for i in range(2 * Q):
            r = gg * 2 * Q + i
            V.tensor_scalar(rows[:, bass.ds((b % 2) * R + r, 1), :], rows[:, bass.ds((b % 2) * R + r, 1), :],
                            m.row[:, bass.ds((b % 2) * 4, 1), bass.ds(r, 1)].rearrange("p a b -> p (a b)"),
                            m.row[:, bass.ds((b % 2) * 4 + 1, 1), bass.ds(r, 1)].rearrange("p a b -> p (a b)"),
                            ALU.subtract, ALU.mult).then_inc(s["norm"], 1)


def load_groups(sp, s, rows, src, gone, credit, per_group):
    for h in range(2):
        sp.sem_inc(s["loaded"][h], 16)

    def load(n, h):
        sp.wait_ge(s["loaded"][h], (n // 2 + 1) * 16)
        sp.dma_start(rows[:, bass.ds((n % (2 * G)) * Q, Q), :],
                     src[bass.ts(n, Q * P), :].rearrange("(q p) c -> p q c", p=P)).then_inc(s["loaded"][h], 16)

    with sp.Fori(0, G, 1) as i:
        for h in range(2):
            load(i * 2 + h, h)
    with sp.Fori(G, BLOCKS * G // 2, 1) as i:
        for h in range(2):
            sp.wait_ge(gone, credit + (i * 2 + h - 2 * G + 1) * per_group)
            load(i * 2 + h, h)


def statistics_buffers(m):
    m.bn = m.sb("bn", [P, R, 6])
    m.dev = m.sb("dev", [P, R])
    m.dev2 = m.sb("dev2", [P, R])
    m.mvc = m.sb("mvc", [P, 2, R])
    m.mT = m.sb("mT", [P, 2, 32])
    m.dT = m.sb("dT", [P, 32])
    m.sum8, m.var8, m.ve, m.msq, m.pow1, m.pow2, m.t8 = (
        m.sb(n, [P, 8]) for n in ("sum8", "var8", "ve", "msq", "pow1", "pow2", "t8"))
    m.tok = m.sb("tok", [P, 4, 8])
    m.tokx = m.sb("tokx", [P, 32, STREAMS])
    m.rowt = m.sb("rowt", [P, 4, R])
    m.row = m.sb("row", [P, 8, R])


def pool_roots(nc, e, m, s, b, rms):
    e.wait_ge(s["ve"], (b * 2 if rms else b) + 1)
    nc.gpsimd.tensor_tensor(m.pow1[:, :], m.ve[:, :], m.minus_half, ALU.pow).then_inc(s["pow"], 1)
    if rms:
        e.wait_ge(s["ve"], b * 2 + 2)
        nc.gpsimd.tensor_tensor(m.pow2[:, :], m.msq[:, :], m.minus_half, ALU.pow).then_inc(s["pow"], 1)


def ffn_program(nc, tag, s, src, dst, consts, w_logit, base, gate, w_branch):
    with ExitStack() as ctx:
        m = Memory(nc, ctx, tag)
        V, A, PE, POOL = nc.vector, nc.scalar, nc.tensor, nc.gpsimd
        const = m.sb("const", [P, C_COLS])
        ident = const[:, C_IDENT:C_IDENT + P]
        sel = const[:, C_SEL:C_SEL + Q * P].rearrange("p (q n) -> p q n", q=Q)
        stream_mask = const[:, C_STREAM:C_STREAM + STREAMS]
        token_mask = const[:, C_TOKEN:C_TOKEN + TPR]
        m.minus_half = const[:, C_HALF:C_HALF + 8]
        statistics_buffers(m)
        xh = m.sb("xh", [P, 2 * R, W])
        wl = m.sb("wl", [P, DT, NL])
        wb = m.sb("wb", [P, KB, W])
        base_b = m.sb("base_b", [P, NL])
        gate_b, ge, gs, g_half, i_half = (
            m.sb(n, [P, 1]) for n in ("gate_b", "ge", "gs", "g_half", "i_half"))
        xT = m.sb("xT", [P, 2, DT, GT])
        lg = m.sb("lg", [P, G, NL])
        z, pr, tmp = (m.sb(n, [P, G, 16]) for n in ("z", "pr", "tmp"))
        uv, luv = (m.sb(n, [P, 2, G, 4]) for n in ("uv", "luv"))
        sm = m.sb("sm", [P, G, 4])
        hp = m.sb("hp", [P, 2 * G, 4])
        hpm = m.sb("hpm", [P, 2 * G])
        h5 = m.sb("h5", [P, G, 5, 4])
        h_post = m.sb("h_post", [P, G, 4])
        rep = m.sb("rep", [P, 2 * G * 5, 4])
        m5 = m.sb("m5", [P, Q, G, 5])
        dsc = m.sb("dsc", [P, R])
        dm = m.sb("dm", [P, Q, G, 4])
        mix_blk = m.sb("mix_blk", [P, 2, Q, TPR, 4])
        pre_blk = m.sb("pre_blk", [P, 2, Q, TPR])
        post_blk = m.sb("post_blk", [P, 2, Q * TPR, 4])
        xpT = m.sb("xpT", [P, KB * GT])
        y_sb = m.sb("y_sb", [P, 2, W])
        o_sb = m.sb("o_sb", [P, 2, Q, W])
        tp = [m.ps(f"tp{i}", [P, W]) for i in range(2)]
        lp = m.ps("lp", [P, NL])
        rp = m.ps("rp", [P, 2 * G * 20])
        xp = m.ps("xp", [P, W])
        yp = m.ps("yp", [P, W])
        op = [m.ps(f"op{i}", [P, W]) for i in range(2)]
        block = ctx.enter_context(nc.Block())

        @block.sync
        def _(sp):
            sp.dma_start(const[:, :], consts).then_inc(s["const"], 16)
            sp.dma_start(wl[:, :, :], w_logit).then_inc(s["weights"], 16)
            sp.dma_start(wb[:, :, :], w_branch).then_inc(s["weights"], 16)
            sp.dma_start(base_b[:, :], base.partition_broadcast(P)).then_inc(s["weights"], 16)
            sp.dma_start(gate_b[:, :], gate.partition_broadcast(P)).then_inc(s["weights"], 16)
            load_groups(sp, s, xh, src, s["o_out"], TWO, Q)

        def row_tile(r, b):
            return xh[:, (b % 2) * R + r, :]

        def row_channels(r, b, k):
            return xh[:, (b % 2) * R + r, k * P:(k + 1) * P]

        @block.gpsimd
        def _(pool):
            pool.wait_ge(s["const"], 16)

            def build(b):
                with pool.Fori(0, G // 2, 1) as gg:
                    for h in range(2):
                        g = gg * 2 + h
                        pool.wait_ge(s["coef"], b + 1)
                        pool.wait_ge(s["blk_free"], b * G + g + 1)
                        POOL.tensor_tensor(
                            pre_blk[:, h, :, :], bcast(token_mask.unsqueeze(1), [P, Q, TPR]),
                            bcast(m5[:, :, bass.ds(g, 1), 4], [P, Q, TPR]), ALU.mult).then_inc(s["pre_blk"], 1)
                        for q in range(Q):
                            POOL.tensor_tensor(
                                mix_blk[:, h, q, :, :], bcast(token_mask.unsqueeze(2), [P, TPR, 4]),
                                bcast(m5[:, q, bass.ds(g, 1), 0:4], [P, TPR, 4]),
                                ALU.mult).then_inc(s["mix_blk"], 1)
                        POOL.tensor_tensor(
                            post_blk[:, h, :, :], bcast(ident.unsqueeze(2), [P, P, 4]),
                            bcast(h_post[:, bass.ds(g, 1), :], [P, P, 4]), ALU.mult).then_inc(s["post_blk"], 1)

            pool_roots(nc, pool, m, s, 0, True)
            with pool.Fori(0, BLOCKS - 1, 1) as b:
                pool_roots(nc, pool, m, s, b + 1, True)
                build(b)
            build(BLOCKS - 1)


        @block.tensor
        def _(pe):
            pe.wait_ge(s["const"], 16)
            pe.wait_ge(s["weights"], 64)
            pe.sem_inc(s["logits"], TWO)
            pe.sem_inc(s["y_full"], ONE)

            def logits(b):
                for g in range(G + 1):
                    n = b * G + g
                    if g < G:
                        pe.wait_ge(s["norm"], n * Q + Q)
                        for k in range(KB):
                            pe.wait_ge(s["xT_in"], n * KB + k + 1)
                            for q in range(Q):
                                mm = PE.transpose(tp[k % 2][:, q * P:(q + 1) * P],
                                                  row_channels(g * Q + q, b, k), ident)
                            mm.then_inc(s["tp_full"], 1)
                    if g >= 1:
                        pe.wait_ge(s["xT_in"], TWO + n * KB)
                        pe.wait_ge(s["lg_in"], n)
                        for d in range(DT):
                            mm = PE.matmul(lp[:, :], xT[:, (g - 1) % 2, d, :], wl[:, d, :],
                                           start=(d == 0), stop=(d == DT - 1))
                        mm.then_inc(s["logits"], 1)

            def coefficients_to_rows(b):
                pe.wait_ge(s["h5"], b + 1)
                for half in range(2):
                    pe.wait_ge(s["rp_free"], b * 2 + half + 1)
                    for q in range(2):
                        mm = PE.matmul(rp[:, q * G * 20:(q + 1) * G * 20], sel[:, half * 2 + q, :],
                                       h5[:, :, :, :].rearrange("p g i j -> p (g i j)"),
                                       start=True, stop=True)
                    mm.then_inc(s["rp_full"], 1)

            def mix(b):
                def pre_mix(g):
                    n = b * G + g
                    pe.wait_ge(s["pre_blk"], n + 1)
                    pe.wait_ge(s["xpT_in"], n + 1)
                    for k in range(KB):
                        for q in range(Q):
                            mm = PE.matmul(xp[:, k * GT + q * TPR:k * GT + (q + 1) * TPR],
                                           row_channels(g * Q + q, b, k), pre_blk[:, g % 2, q, :],
                                           start=True, stop=True)
                    mm.then_inc(s["xp_full"], 1)

                def branch(g):
                    n = b * G + g
                    pe.wait_ge(s["xpT_in"], ONE + n + 1)
                    pe.wait_ge(s["y_in"], n + 1)
                    for k in range(KB):
                        mm = PE.matmul(yp[:, :], xpT[:, k * GT:(k + 1) * GT], wb[:, k, :],
                                       start=(k == 0), stop=(k == KB - 1))
                    mm.then_inc(s["y_full"], 1)

                def mix_rows(g, q):
                    n = b * G + g
                    if q == 0:
                        pe.wait_ge(s["mix_blk"], n * Q + Q)
                        pe.wait_ge(s["post_blk"], ONE + n + 1)
                        pe.wait_ge(s["y_in"], ONE + n + 1)
                    pe.wait_ge(s["o_out"], n * Q + q + 1)
                    PE.matmul(op[q % 2][:, :], mix_blk[:, g % 2, q, :, :].rearrange("p t i -> p (t i)"),
                              row_tile(g * Q + q, b), start=True, stop=False)
                    PE.matmul(op[q % 2][:, :], post_blk[:, g % 2, q * TPR:(q + 1) * TPR, :]
                              .rearrange("p t i -> p (t i)"), y_sb[:, g % 2, :],
                              start=False, stop=True).then_inc(s["o_full"], 1)

                pre_mix(0)
                branch(0)
                for g in range(G):
                    if g + 1 < G:
                        pre_mix(g + 1)
                    mix_rows(g, 0)
                    mix_rows(g, 1)
                    if g + 1 < G:
                        branch(g + 1)
                    mix_rows(g, 2)
                    mix_rows(g, 3)

            logits(0)
            for b in range(BLOCKS):
                coefficients_to_rows(b)
                if b + 1 < BLOCKS:
                    logits(b + 1)
                mix(b)

        @block.scalar
        def _(act):
            act.preload_act_table_set(EXP_AND_LN)
            act.wait_ge(s["weights"], 64)
            A.activation(ge[:, :], gate_b[:, :], ACT.Exp, scale=-1.0).then_inc(s["gate"], 1)
            act.sem_inc(s["xT_in"], TWO)
            act.sem_inc(s["xpT_in"], ONE)
            act.sem_inc(s["y_in"], ONE)
            act.sem_inc(s["o_out"], TWO)
            act.sem_inc(s["blk_free"], TWO)
            act.sem_inc(s["stored"][0], 16)
            act.sem_inc(s["stored"][1], 16)

            def transposed(b):
                with act.Fori(0, G // 2, 1) as gg:
                    for h in range(2):
                        n = b * G + gg * 2 + h
                        act.wait_ge(s["logits"], n + 1)
                        for k in range(KB):
                            act.wait_ge(s["tp_full"], n * KB + k + 1)
                            A.activation(xT[:, h, k::KB, :],
                                         tp[k % 2][:, :].rearrange("p (n j) -> p j n", j=STREAMS),
                                         ACT.Copy).then_inc(s["xT_in"], 1)

            def softmax_functions(b):
                for i, (out, in_, f) in enumerate(
                        [(hp[:, :, :], hp[:, :, :], ACT.Exp)]
                        + [(tmp[:, :, :], z[:, :, :], ACT.Exp), (sm[:, :, :], sm[:, :, :], ACT.Ln)] * 2
                        + [(pr[:, :, :], z[:, :, :], ACT.Exp)]):
                    act.wait_ge(s["ask"], b * ASKS + i + 1)
                    A.activation(out, in_, f).then_inc(s["given"], 1)

            def absorb_functions(b, a):
                act.wait_ge(s["ask"], b * ASKS + 6 + a * 2 + 1)
                A.activation(luv[:, :, :, :], uv[:, :, :, :], ACT.Ln).then_inc(s["given"], 1)
                act.wait_ge(s["ask"], b * ASKS + 6 + a * 2 + 2)
                A.activation(pr[:, :, :], z[:, :, :], ACT.Exp).then_inc(s["given"], 1)

            def pre_mixed(b, g):
                n = b * G + g
                act.wait_ge(s["xp_full"], n + 1)
                act.wait_ge(s["y_full"], n + 1)
                A.activation(xpT[:, :], xp[:, :], ACT.Copy).then_inc(s["xpT_in"], 1)

            def branched(b, g, h):
                act.wait_ge(s["y_full"], ONE + b * G + g + 1)
                A.activation(y_sb[:, h, :], yp[:, :], ACT.Copy).then_inc(s["y_in"], 1)

            def mixed(b, g, h):
                n = b * G + g
                if g + 1 < G:
                    pre_mixed(b, g + 1)
                act.wait_ge(s["stored"][h], (b * (G // 2) + (g - h) // 2 + 1) * 16)
                for q in range(Q):
                    if q == 2 and g + 1 < G:
                        branched(b, g + 1, 1 - h)
                    act.wait_ge(s["o_full"], n * Q + q + 1)
                    A.activation(o_sb[:, h, q, :], op[q % 2][:, :], ACT.Identity,
                                 bias=m.row[:, bass.ds((b % 2) * 4, 1), bass.ds(g * Q + q, 1)]
                                 .rearrange("p a b -> p (a b)")).then_inc(s["o_out"], 1)
                act.sem_inc(s["blk_free"], 1)
                act.wait_ge(s["o_out"], TWO + n * Q + Q)
                act.dma_start(dst[bass.ts(n, Q * P), :].rearrange("(q p) c -> p q c", p=P),
                              o_sb[:, h, :, :]).then_inc(s["stored"][h], 16)

            transposed(0)
            softmax_functions(0)
            with act.Fori(0, ABSORBS, 1) as a:
                absorb_functions(0, a)
            with act.Fori(0, BLOCKS - 1, 1) as b:
                transposed(b + 1)
                pre_mixed(b, 0)
                branched(b, 0, 0)
                mixed(b, 0, 0)
                softmax_functions(b + 1)
                for g in range(1, G):
                    mixed(b, g, g % 2)
                    absorb_functions(b + 1, g - 1)
            pre_mixed(BLOCKS - 1, 0)
            branched(BLOCKS - 1, 0, 0)
            for g in range(G):
                mixed(BLOCKS - 1, g, g % 2)
            for h in range(2):
                act.wait_ge(s["stored"][h], 16 + 16 * BLOCKS * G // 2)

        @block.vector
        def _(dve):
            dve.wait_ge(s["weights"], 64)
            dve.wait_ge(s["const"], 16)
            dve.sem_inc(s["lg_in"], ONE)
            dve.sem_inc(s["rp_free"], ONE)
            dve.sem_inc(s["post_blk"], ONE)
            c0 = Chain(dve, s["setup"], 0)
            dve.wait_ge(s["gate"], 1)
            c0.then(V.tensor_scalar(gs[:, :], ge[:, :], 1.0, None, ALU.add))
            c0.then(V.reciprocal(ge[:, :], gs[:, :]))
            c0.then(V.tensor_scalar(g_half[:, :], ge[:, :], 0.5, None, ALU.mult))
            c0.then(V.tensor_scalar(i_half[:, :], ge[:, :], -0.5, 0.5, ALU.mult, ALU.add))
            g4 = [P, G, 4, 4]

            def by_row(t):
                return t[:, :, :].rearrange("p g (i j) -> p g i j", i=4)

            def by_col(t):
                return t[:, :, :].rearrange("p g (i j) -> p g j i", i=4)

            def over(v):
                return bcast(v.unsqueeze(3), g4)

            with dve.Fori(0, BLOCKS, 1) as b:
                row_statistics(nc, dve, m, s, xh, b, True)
                with dve.Fori(0, G, 1) as g:
                    dve.wait_ge(s["logits"], TWO + b * G + g + 1)
                    V.tensor_tensor(lg[:, bass.ds(g, 1), :], lp[:, :].unsqueeze(1),
                                    base_b[:, :].unsqueeze(1), ALU.add).then_inc(s["lg_in"], 1)
                dve.wait_ge(s["lg_in"], ONE + b * G + G)

                c = Chain(dve, s["sink"], b * STEPS)
                asked = 0

                def ask(ins):
                    nonlocal asked
                    ins.then_inc(s["ask"], 1)
                    asked += 1
                    dve.wait_ge(s["given"], b * ASKS + asked)

                pp = lg[:, :, 16:24].rearrange("p g (s n) -> p g s n", s=2)
                hv = hp[:, :, :].rearrange("p (g s) n -> p g s n", s=2)
                c.then(V.tensor_reduce(hpm[:, :], pp, AX.X, ALU.max))
                ask(V.tensor_tensor(hv, pp, bcast(hpm[:, :].rearrange("p (g s) -> p g s", s=2)
                                                  .unsqueeze(3), [P, G, 2, 4]), ALU.subtract))
                c.then(V.tensor_reduce(hpm[:, :], hp[:, :, :], AX.X, ALU.add))
                c.then(V.reciprocal(hpm[:, :], hpm[:, :]))
                c.then(V.tensor_tensor(hp[:, :, :], hp[:, :, :],
                                       bcast(hpm[:, :].unsqueeze(2), [P, 2 * G, 4]), ALU.mult))
                c.then(V.tensor_scalar(z[:, :, :], lg[:, :, 0:16], TAU_INV, None, ALU.mult))
                for view in (by_row, by_col):
                    c.then(V.tensor_reduce(sm[:, :, :], view(z), AX.X, ALU.max))
                    ask(V.tensor_tensor(view(z), view(z), over(sm[:, :, :]), ALU.subtract))
                    ask(V.tensor_reduce(sm[:, :, :], view(tmp), AX.X, ALU.add))
                    ins = V.tensor_tensor(view(z), view(z), over(sm[:, :, :]), ALU.subtract)
                    if view is by_row:
                        c.then(ins)
                ins.then_inc(s["ask"], 1)
                first = c.steps
                with dve.Fori(0, ABSORBS, 1) as a:
                    dve.wait_ge(s["given"], b * ASKS + 6 + a * 2)
                    ca = Chain(dve, s["sink"], b * STEPS + first + a * (6 * ITERS_PER_ABSORB - 1))
                    for i in range(ITERS_PER_ABSORB):
                        if i:
                            ca.then(V.tensor_tensor(by_row(tmp), by_row(pr),
                                                    bcast(uv[:, 1, :, :].unsqueeze(2), g4), ALU.mult))
                        ca.then(V.tensor_reduce(sm[:, :, :], by_row(tmp if i else pr), AX.X, ALU.add))
                        ca.then(V.reciprocal(uv[:, 0, :, :], sm[:, :, :]))
                        ca.then(V.tensor_tensor(by_row(tmp), by_row(pr), over(uv[:, 0, :, :]), ALU.mult))
                        ca.then(V.tensor_reduce(sm[:, :, :], by_col(tmp), AX.X, ALU.add))
                        ins = V.reciprocal(uv[:, 1, :, :], sm[:, :, :])
                        if i < ITERS_PER_ABSORB - 1:
                            ca.then(ins)
                    ins.then_inc(s["ask"], 1)
                    dve.wait_ge(s["given"], b * ASKS + 6 + a * 2 + 1)
                    ca.then(V.tensor_tensor(by_row(z), by_row(z), over(luv[:, 0, :, :]), ALU.add))
                    V.tensor_tensor(by_row(z), by_row(z), bcast(luv[:, 1, :, :].unsqueeze(2), g4),
                                    ALU.add).then_inc(s["ask"], 1)
                    assert ca.steps == 6 * ITERS_PER_ABSORB - 1, ca.steps
                c.steps += (6 * ITERS_PER_ABSORB - 1) * ABSORBS
                dve.wait_ge(s["given"], b * ASKS + ASKS)
                dve.wait_ge(s["post_blk"], b * G + 1)
                c.done(V.tensor_copy(h5[:, :, 4, :], hv[:, :, 0, :]))
                c.done(V.tensor_scalar(h_post[:, :, :], hv[:, :, 1, :], 0.5, None, ALU.mult))
                V.tensor_scalar(h5[:, :, 0:4, :].rearrange("p g i j -> p g (i j)"), pr[:, :, :],
                                g_half[:, 0:1], None, ALU.mult).then_inc(s["h5"], 1)
                for half in range(2):
                    dve.wait_ge(s["rp_full"], b * 2 + half + 1)
                    c.then(V.tensor_tensor(rep[:, :, :], rp[:, :].rearrange("p (n j) -> p n j", j=4),
                                           bcast(stream_mask.unsqueeze(1), [P, 2 * G * 5, 4]), ALU.mult))
                    dve.sem_inc(s["rp_free"], 1)
                    c.then(V.tensor_reduce(m5[:, 2 * half:2 * half + 2, :, :].rearrange("p q g i -> p (q g i)"),
                                           rep[:, :, :], AX.X, ALU.add))
                slot = (b % 2) * 4
                ms = m.row[:, bass.ds(slot + 2, 1), :].rearrange("p a r -> p (a r)")
                std = m.row[:, bass.ds(slot + 3, 1), :].rearrange("p a r -> p (a r)")
                c.then(V.tensor_tensor(m5[:, :, :, :], m5[:, :, :, :], bcast(
                    ms.rearrange("p (g q) -> p q g", q=Q).unsqueeze(3), [P, Q, G, 5]), ALU.mult))
                c.then(V.scalar_tensor_tensor(dsc[:, :], ms, i_half[:, 0:1], std, ALU.mult, ALU.add))
                c.then(V.tensor_tensor(dm[:, :, :, :],
                                       bcast(dsc[:, :].rearrange("p (g q) -> p q g", q=Q).unsqueeze(3), [P, Q, G, 4]),
                                       bcast(stream_mask.unsqueeze(1).unsqueeze(1), [P, Q, G, 4]), ALU.mult))
                V.tensor_tensor(m5[:, :, :, 0:4], m5[:, :, :, 0:4], dm[:, :, :, :], ALU.add).then_inc(s["coef"], 1)
                assert asked == 5 and c.steps == STEPS, (asked, c.steps)


FFN_SIGNALS = ["const", "weights", "coef", "blk_free", "pre_blk", "mix_blk", "post_blk", "norm",
               "tp_full", "xT_in", "logits", "lg_in", "h5", "rp_free", "rp_full", "xp_full", "xpT_in",
               "y_full", "y_in", "o_full", "o_out", "gate", "ask", "given", "setup", "sink",
               "bn", "stat", "ve", "pow", "row"]


def project_program(nc, tag, s, src, normed, projected, consts, w_proj):
    with ExitStack() as ctx:
        m = Memory(nc, ctx, tag)
        V, A, PE = nc.vector, nc.scalar, nc.tensor
        const = m.sb("const", [P, C_COLS])
        ident = const[:, C_IDENT:C_IDENT + P]
        m.minus_half = const[:, C_HALF:C_HALF + 8]
        statistics_buffers(m)
        xh = m.sb("xh", [P, 2 * R, W])
        wp = m.sb("wp", [P, DT, NP])
        CG = T // GT
        xT = m.sb("xT", [P, DT, 2, T])
        proj = m.sb("proj", [NP, T])
        tp = [m.ps(f"tp{i}", [P, W]) for i in range(4)]
        pp = [m.ps(f"pp{i}", [NP, T]) for i in range(2)]
        block = ctx.enter_context(nc.Block())
        FOUR = len(tp)

        @block.sync
        def _(sp):
            sp.dma_start(const[:, :], consts).then_inc(s["const"], 16)
            sp.dma_start(wp[:, :, :], w_proj).then_inc(s["weights"], 16)
            load_groups(sp, s, xh, src, s["tp_full"], 0, KB)

        @block.gpsimd
        def _(pool):
            pool.wait_ge(s["const"], 16)
            for b in range(BLOCKS):
                pool_roots(nc, pool, m, s, b, False)

        @block.vector
        def _(dve):
            dve.wait_ge(s["const"], 16)
            with dve.Fori(0, BLOCKS, 1) as b:
                row_statistics(nc, dve, m, s, xh, b, False)


        @block.tensor
        def _(pe):
            pe.wait_ge(s["const"], 16)
            pe.wait_ge(s["weights"], 16)
            for b in range(BLOCKS):
                for g in range(G):
                    n = b * G + g
                    pe.wait_ge(s["norm"], n * Q + Q)
                    for k in range(KB):
                        pe.wait_ge(s["xT_in"], n * KB + k + 1)
                        for q in range(Q):
                            mm = PE.transpose(tp[k][:, q * P:(q + 1) * P],
                                              xh[:, (b % 2) * R + g * Q + q, k * P:(k + 1) * P], ident)
                        mm.then_inc(s["tp_full"], 1)
                    if g % CG == CG - 1:
                        c = n // CG
                        pe.wait_ge(s["xT_in"], FOUR + (n + 1) * KB)
                        pe.wait_ge(s["proj_in"], c + 1)
                        for d in range(DT):
                            mm = PE.matmul(pp[c % 2][:, :], wp[:, d, :], xT[:, d, c % 2, :],
                                           start=(d == 0), stop=(d == DT - 1))
                        mm.then_inc(s["proj_full"], 1)

        @block.scalar
        def _(act):
            act.sem_inc(s["xT_in"], FOUR)
            act.sem_inc(s["proj_in"], TWO)
            act.sem_inc(s["stored"][0], 16)
            act.sem_inc(s["stored"][0], 16)
            act.sem_inc(s["stored"][1], 16)
            with act.Fori(0, CHUNKS // 2, 1) as cc:
                for h in range(2):
                    c = cc * 2 + h
                    for g in range(CG):
                        n = c * CG + g
                        for k in range(KB):
                            act.wait_ge(s["tp_full"], n * KB + k + 1)
                            if g == 0 and k == 0:
                                act.wait_ge(s["stored"][0], (c + 1) * 16)
                                act.wait_ge(s["proj_in"], c + 1)
                            A.activation(xT[:, k::KB, h, g * GT:(g + 1) * GT],
                                         tp[k][:, :].rearrange("p (n j) -> p j n", j=STREAMS),
                                         ACT.Copy).then_inc(s["xT_in"], 1)
                    act.wait_ge(s["xT_in"], FOUR + (c + 1) * CG * KB)
                    act.dma_start(normed[bass.ts(c, DT * P), :].rearrange("(d p) t -> p d t", p=P),
                                  xT[:, :, h, :]).then_inc(s["stored"][0], 16)
                    act.wait_ge(s["proj_full"], c + 1)
                    act.wait_ge(s["stored"][1], (c + 1) * 16)
                    A.activation(proj[:, :], pp[h][:, :], ACT.Copy).then_inc(s["proj_in"], 1)
                    act.wait_ge(s["proj_in"], TWO + c + 1)
                    act.dma_start(projected[:, bass.ts(c, T)], proj[:, :]).then_inc(s["stored"][1], 16)
            act.wait_ge(s["stored"][0], 32 + 16 * CHUNKS)
            act.wait_ge(s["stored"][1], 16 + 16 * CHUNKS)


PROJECT_SIGNALS = ["const", "weights", "norm", "tp_full", "xT_in", "proj_full", "proj_in",
                   "bn", "stat", "ve", "pow", "row"]

C_CHAN = S + 2
HSLOTS = 8
GSLOTS = 4
ASLOTS = 3
K = CHUNKS * DT


def scan_program(nc, tag, s, x_in, normed, projected, x_out, consts, channels, w_dt, keep):
    with ExitStack() as ctx:
        m = Memory(nc, ctx, tag)
        V, A, PE, POOL = nc.vector, nc.scalar, nc.tensor, nc.gpsimd
        ident = m.sb("ident", [P, P])
        keep_sb = m.sb("keep", [P, K])
        bc = m.sb("bc", [P, 2, 2 * S, T])
        dt_in = m.sb("dt_in", [RANK, 2, T])
        xn = m.sb("xn", [P, 2, T])
        x_blk = m.sb("x_blk", [P, 2, T // P, P])
        chan = m.sb("chan", [P, 2, C_CHAN])
        wdt = m.sb("wdt", [RANK, 2, P])
        neg_a = m.sb("neg_a", [P, 2, S])
        mag, ex, rl, ln1p = (m.sb(n, [P, T]) for n in ("mag", "ex", "rl", "ln1p"))
        neg_dt = m.sb("neg_dt", [P, 2, T])
        diag_d = m.sb("diag_d", [P, 2, P])
        h_last = m.sb("h_last", [P, DT, S])
        h_first = m.sb("h_first", [P, 2, S])
        bx = m.sb("bx", [P, ASLOTS, T])
        hs = m.sb("hs", [P, HSLOTS, T])
        ch = m.sb("ch", [P, GSLOTS, T])
        y_sb = m.sb("y_sb", [P, T])
        o_sb = m.sb("o_sb", [P, 2, T // P, P])
        decay = [m.ps(f"decay{i}", [P, T]) for i in range(ASLOTS)]
        u = m.ps("u", [P, T])
        acc = [m.ps(f"acc{i}", [P, T]) for i in range(2)]
        dt_raw = m.ps("dt_raw", [P, T])
        turned = m.ps("turned", [P, T])
        block = ctx.enter_context(nc.Block())
        x_tok = x_in.rearrange("(n j) c -> n (j c)", j=STREAMS)
        out_tok = x_out.rearrange("(n j) c -> n (j c)", j=STREAMS)

        def token_block(x, k):
            return x[bass.ds((k // DT) * T, T), bass.ds((k % DT) * P, P)].rearrange("(a p) c -> p a c", p=P)

        def reuse(n):
            return ASLOTS if n == 0 else 1


        @block.sync
        def _(sp):
            def load(k, h):
                sp.wait_ge(s["diag"], k + 1)
                sp.dma_start(chan[:, h, :], channels[bass.ts(k % DT, P), :]).then_inc(s["params"][h], 16)
                sp.dma_start(wdt[:, h, :], w_dt[bass.ts(k % DT, RANK), :]).then_inc(s["params"][h], 16)
                sp.wait_ge(s["skip"], k + 1)
                sp.dma_start(xn[:, h, :], normed[bass.ts(k, P), :]).then_inc(s["xn"][h], 16)
                sp.wait_ge(s["turned"], k + 1)
                sp.dma_start(x_blk[:, h, :, :], token_block(x_tok, k)).then_inc(s["x_blk"][h], 16)

            def load_chunk(c):
                sp.dma_start(dt_in[:, bass.ds(c % 2, 1), :],
                             projected[0:RANK, bass.ts(c, T)].unsqueeze(1)).then_inc(s["chunk"], 16)
                sp.dma_start(bc[:, bass.ds(c % 2, 1), :, :],
                             projected[RANK:NP, bass.ts(c, T)].unsqueeze(0).partition_broadcast(P)
                             ).then_inc(s["chunk"], 16)

            sp.dma_start(ident[:, :], consts[:, C_IDENT:C_IDENT + P]).then_inc(s["const"], 16)
            sp.dma_start(keep_sb[:, :], keep).then_inc(s["const"], 16)
            load_chunk(0)
            with sp.Fori(0, CHUNKS - 1, 1) as c:
                for h in range(2):
                    load(c * DT + h, h)
                sp.wait_ge(s["chunk"], c * 32 + 32)
                sp.wait_ge(s["scaled"], HSLOTS + c * DT * S)
                load_chunk(c + 1)
                with sp.Fori(1, DT // 2, 1) as i:
                    for h in range(2):
                        load(c * DT + i * 2 + h, h)
            with sp.Fori(0, DT // 2, 1) as i:
                for h in range(2):
                    load((CHUNKS - 1) * DT + i * 2 + h, h)

        @block.scalar
        def _(act):
            act.preload_act_table_set(EXP_AND_LN)
            act.sem_inc(s["dt_read"], ONE)
            act.sem_inc(s["y_in"], ONE)
            act.sem_inc(s["turned_in"], ONE)
            act.sem_inc(s["stored"][0], 16)
            act.sem_inc(s["stored"][1], 16)

            def softplus(k, h):
                act.wait_ge(s["params"][h], (k // 2) * 32 + 32)
                A.activation(neg_a[:, h, :], chan[:, h, 0:S], ACT.Exp).then_inc(s["neg_a"], 1)
                act.wait_ge(s["dt_raw"], k + 1)
                A.activation(mag[:, :], dt_raw[:, :], ACT.Abs, bias=chan[:, h, S + 1:S + 2]).then_inc(s["soft"], 1)
                act.wait_ge(s["neg_dt"], k + 1)
                A.activation(rl[:, :], dt_raw[:, :], ACT.Relu, bias=chan[:, h, S + 1:S + 2]).then_inc(s["dt_read"], 1)
                act.wait_ge(s["soft"], k * 3 + 1)
                A.activation(ex[:, :], mag[:, :], ACT.Exp, scale=-1.0).then_inc(s["soft"], 1)
                act.wait_ge(s["soft"], k * 3 + 2)
                A.activation(ln1p[:, :], ex[:, :], ACT.Ln, bias=1.0).then_inc(s["soft"], 1)

            def step(k, h, first=False, last=False):
                act.wait_ge(s["neg_a"], k + 1)
                act.wait_ge(s["neg_dt"], ONE + k + 1)
                for n in range(S):
                    U = k * S + n
                    act.wait_ge(s["scan"], U + reuse(n))
                    A.activation(decay[n % ASLOTS][:, :], neg_dt[:, h, :], ACT.Exp,
                                 scale=neg_a[:, h, n:n + 1]).then_inc(s["decay"], 1)
                    if n == 6 and not first:
                        copy_sum(k - 1, 1 - h)
                    if n == 9 and not last:
                        softplus(k + 1, 1 - h)
                    if n == 12 and not first:
                        copy_turned(k - 1, 1 - h)

            def copy_sum(k, h):
                act.wait_ge(s["summed"], GSLOTS + (k + 1) * S)
                act.wait_ge(s["turned"], TWO + k)
                A.activation(y_sb[:, :], acc[h][:, :], ACT.Copy).then_inc(s["y_in"], 1)

            def copy_turned(k, h):
                act.wait_ge(s["turned"], TWO + k + 1)
                act.wait_ge(s["stored"][h], (k // 2) * 16 + 16)
                A.activation(o_sb[:, h, :, :].rearrange("p a c -> p (a c)"), turned[:, :],
                             ACT.Copy).then_inc(s["turned_in"], 1)
                act.wait_ge(s["turned_in"], ONE + k + 1)
                act.dma_start(token_block(out_tok, k), o_sb[:, h, :, :]).then_inc(s["stored"][h], 16)

            softplus(0, 0)
            step(0, 0, first=True)
            with act.Fori(0, (K - 2) // 2, 1) as i:
                step(i * 2 + 1, 1)
                step(i * 2 + 2, 0)
            step(K - 1, 1, last=True)
            copy_sum(K - 1, 1)
            copy_turned(K - 1, 1)
            for h in range(2):
                act.wait_ge(s["stored"][h], 16 + 16 * K // 2)

        @block.vector
        def _(dve):
            dve.memset(h_last[:, :, :], 0.0).then_inc(s["state"], 1)
            dve.sem_inc(s["scan"], ASLOTS)
            dve.sem_inc(s["neg_dt"], ONE)
            dve.sem_inc(s["bx"], ONE)
            dve.sem_inc(s["diag"], TWO)
            dve.wait_ge(s["const"], 32)

            def make_neg_dt(k, h):
                dve.wait_ge(s["soft"], k * 3 + 3)
                dve.wait_ge(s["dt_read"], ONE + k + 1)
                V.scalar_tensor_tensor(neg_dt[:, h, :], rl[:, :], -1.0, ln1p[:, :],
                                       ALU.mult, ALU.subtract).then_inc(s["neg_dt"], 1)
                V.tensor_scalar(diag_d[:, h, :], ident[:, :], chan[:, h, S:S + 1], None,
                                ALU.mult).then_inc(s["diag"], 1)

            def make_u(k, h):
                dve.wait_ge(s["neg_dt"], ONE + k + 1)
                dve.wait_ge(s["xn"][h], (k // 2) * 16 + 16)
                dve.wait_ge(s["bx"], ONE + k * S)
                V.scalar_tensor_tensor(u[:, :], neg_dt[:, h, :], -1.0, xn[:, h, :],
                                       ALU.mult, ALU.mult).then_inc(s["u"], 1)

            def step(k, h, first=False, last=False):
                slot = (k // DT) % 2

                def make_input(n):
                    U = k * S + n
                    dve.wait_ge(s["scan"], U + reuse(n))
                    V.tensor_tensor(bx[:, n % ASLOTS, :], u[:, :], bc[:, bass.ds(slot, 1), n, :]
                                    .rearrange("p a t -> p (a t)"), ALU.mult).then_inc(s["bx"], 1)

                def scan(n):
                    U = k * S + n
                    if n == 0:
                        dve.wait_ge(s["first"], k + 1)
                    if n == HSLOTS:
                        dve.wait_ge(s["state"], k * 2 + 2)
                    dve.wait_ge(s["scaled"], U + 1)
                    dve.wait_ge(s["decay"], U + 1)
                    dve.wait_ge(s["bx"], ONE + U + 1)
                    V.tensor_tensor_scan(hs[:, n % HSLOTS, :], decay[n % ASLOTS][:, :], bx[:, n % ASLOTS, :],
                                         h_first[:, h, n:n + 1], ALU.mult, ALU.add).then_inc(s["scan"], 1)

                def save(k, half):
                    dve.wait_ge(s["scan"], ASLOTS + k * S + (half + 1) * HSLOTS)
                    V.tensor_scalar(h_last[:, bass.ds(k % DT, 1), half * HSLOTS:(half + 1) * HSLOTS],
                                    hs[:, :, T - 1].unsqueeze(1), 1.0, None, ALU.mult).then_inc(s["state"], 1)

                dve.wait_ge(s["chunk"], (k // DT) * 32 + 32)
                dve.wait_ge(s["u"], k + 1)
                make_input(0)
                if not first:
                    save(k - 1, 1)
                make_input(1)
                dve.wait_ge(s["state"], k * 2 + 1)
                V.tensor_scalar(h_first[:, h, :], h_last[:, bass.ds(k % DT, 1), :].rearrange("p a n -> p (a n)"),
                                keep_sb[:, bass.ds(k, 1)], None, ALU.mult).then_inc(s["first"], 1)
                for n in range(S):
                    if 1 <= n < S - 1:
                        make_input(n + 1)
                    if n == HSLOTS:
                        save(k, 0)
                    if n == S - 2 and not last:
                        make_neg_dt(k + 1, 1 - h)
                    if n == S - 1 and not last:
                        make_u(k + 1, 1 - h)
                    scan(n)

            make_neg_dt(0, 0)
            make_u(0, 0)
            step(0, 0, first=True)
            with dve.Fori(0, (K - 2) // 2, 1) as i:
                step(i * 2 + 1, 1)
                step(i * 2 + 2, 0)
            step(K - 1, 1, last=True)

        @block.gpsimd
        def _(pool):
            pool.sem_inc(s["scaled"], HSLOTS)
            with pool.Fori(0, K // 2, 1) as i:
                for h in range(2):
                    k = i * 2 + h
                    for n in range(S):
                        U = k * S + n
                        pool.wait_ge(s["summed"], U + 1)
                        pool.wait_ge(s["scan"], ASLOTS + U + 1)
                        POOL.tensor_tensor(ch[:, n % GSLOTS, :], hs[:, n % HSLOTS, :],
                                           bc[:, bass.ds((k // DT) % 2, 1), S + n, :]
                                           .rearrange("p a t -> p (a t)"), ALU.mult).then_inc(s["scaled"], 1)

        @block.tensor
        def _(pe):
            pe.sem_inc(s["summed"], GSLOTS)
            pe.sem_inc(s["turned"], TWO)
            pe.sem_inc(s["skip"], TWO)
            pe.wait_ge(s["const"], 32)

            def raw_dt(k, h):
                pe.wait_ge(s["params"][h], (k // 2) * 32 + 32)
                pe.wait_ge(s["chunk"], (k // DT) * 32 + 32)
                pe.wait_ge(s["dt_read"], k + 1)
                PE.matmul(dt_raw[:, :], wdt[:, h, :], dt_in[:, bass.ds((k // DT) % 2, 1), :]
                          .rearrange("p a t -> p (a t)"), start=True, stop=True).then_inc(s["dt_raw"], 1)

            def turn(k, h):
                pe.wait_ge(s["turned_in"], k + 1)
                pe.wait_ge(s["y_in"], ONE + k + 1)
                pe.wait_ge(s["x_blk"][h], (k // 2) * 16 + 16)
                PE.matmul(turned[:, :], ident[:, :], x_blk[:, h, :, :].rearrange("p a c -> p (a c)"),
                          start=True, stop=False)
                for a in range(T // P):
                    mm = PE.matmul(turned[:, a * P:(a + 1) * P], y_sb[:, a * P:(a + 1) * P], ident[:, :],
                                   start=False, stop=(a == T // P - 1))
                mm.then_inc(s["turned"], 1)

            def step(k, h, first=False, last=False):
                pe.wait_ge(s["diag"], TWO + k + 1)
                pe.wait_ge(s["u"], k + 1)
                pe.wait_ge(s["xn"][h], (k // 2) * 16 + 16)
                if not first:
                    pe.wait_ge(s["y_in"], k)
                PE.matmul(acc[h][:, :], diag_d[:, h, :], xn[:, h, :], start=True,
                          stop=False).then_inc(s["skip"], 1)
                for n in range(S):
                    pe.wait_ge(s["scaled"], HSLOTS + k * S + n + 1)
                    mm = PE.matmul(acc[h][:, :], ident[:, :], ch[:, n % GSLOTS, :],
                                   start=False, stop=(n == S - 1))
                    mm.then_inc(s["summed"], 1)
                    if n == 2 and not last:
                        raw_dt(k + 1, 1 - h)
                    if n == 5 and not first:
                        turn(k - 1, 1 - h)

            raw_dt(0, 0)
            step(0, 0, first=True)
            with pe.Fori(0, (K - 2) // 2, 1) as i:
                step(i * 2 + 1, 1)
                step(i * 2 + 2, 0)
            step(K - 1, 1, last=True)
            turn(K - 1, 1)


SCAN_SIGNALS = ["const", "chunk", "turned", "dt_read", "y_in", "turned_in", "neg_a", "dt_raw", "soft",
                "neg_dt", "scan", "decay", "state", "first", "skip", "diag", "bx", "u", "scaled", "summed"]


def build(nc, x, w_logit, base, gate, w_branch, w_proj, channels, w_dt, consts, keep, out):
    def scratch(name, shape):
        return nc.dram_tensor(name, shape, F32, kind="Internal").ap()

    x1, x2 = (scratch(n, [TOKENS * STREAMS, W]) for n in ("x1", "x2"))
    normed = scratch("normed", [K * P, T])
    projected = scratch("projected", [NP, TOKENS])
    with ExitStack() as ctx:
        ffn1, ffn2 = (signals(nc, ctx, n, FFN_SIGNALS, ("stored", "loaded")) for n in ("ffn1", "ffn2"))
        project = signals(nc, ctx, "project", PROJECT_SIGNALS, ("stored", "loaded"))
        scan = signals(nc, ctx, "scan", SCAN_SIGNALS, ("stored", "params", "xn", "x_blk"))
        ffn_program(nc, "ffn1", ffn1, x, x1, consts, w_logit, base, gate, w_branch)
        project_program(nc, "project", project, x1, normed, projected, consts, w_proj)
        scan_program(nc, "scan", scan, x1, normed, projected, x2, consts, channels, w_dt, keep)
        ffn_program(nc, "ffn2", ffn2, x2, out, consts, w_logit, base, gate, w_branch)


def constants():
    import numpy as np
    p = np.arange(P)
    c = np.zeros((P, C_COLS), np.float32)
    c[:, C_IDENT:C_IDENT + P] = p[:, None] == p[None, :]
    for q in range(Q):
        c[:, C_SEL + q * P:C_SEL + (q + 1) * P] = p[:, None] == q * TPR + p[None, :] // STREAMS
    c[:, C_STREAM:C_STREAM + STREAMS] = p[:, None] % STREAMS == np.arange(STREAMS)
    c[:, C_TOKEN:C_TOKEN + TPR] = p[:, None] // STREAMS == np.arange(TPR)
    c[:, C_HALF:] = -0.5
    keep = np.ones((P, K), np.float32)
    keep[:, np.arange(K) // DT % CPB == 0] = 0.0
    return c, keep


def kernel(L0_attn_x, L0_attn_A_log, L0_attn_D, L0_attn_x_proj_w, L0_attn_dt_proj_w, L0_attn_dt_proj_b,
           L0_ffn_W_res, L0_ffn_W_pre, L0_ffn_W_post, L0_ffn_H_res_base, L0_ffn_H_pre_base,
           L0_ffn_H_post_base, L0_ffn_gate, L0_ffn_W_branch):
    import numpy as np
    import concourse.bacc as bacc
    from concourse.bass_utils import run_bass_kernel_spmd

    def tiles(w):
        return np.ascontiguousarray(w.T.reshape(-1, P, w.shape[0]).transpose(1, 0, 2))

    consts, keep = constants()
    arrays = {
        "x": np.ascontiguousarray(L0_attn_x).reshape(TOKENS * STREAMS, W),
        "w_logit": tiles(np.concatenate([L0_ffn_W_res, L0_ffn_W_pre, L0_ffn_W_post])),
        "base": np.concatenate([np.asarray(L0_ffn_H_res_base).reshape(-1), L0_ffn_H_pre_base, L0_ffn_H_post_base]),
        "gate": np.ascontiguousarray(L0_ffn_gate),
        "w_branch": np.ascontiguousarray(np.asarray(L0_ffn_W_branch).reshape(KB, P, W).transpose(1, 0, 2)),
        "w_proj": tiles(np.asarray(L0_attn_x_proj_w)),
        "channels": np.concatenate([L0_attn_A_log, np.asarray(L0_attn_D)[:, None],
                                    np.asarray(L0_attn_dt_proj_b)[:, None]], axis=1),
        "w_dt": np.ascontiguousarray(np.asarray(L0_attn_dt_proj_w).reshape(DT, P, RANK)
                                     .transpose(0, 2, 1)).reshape(DT * RANK, P),
        "consts": consts,
        "keep": keep,
    }
    nc = bacc.Bacc("TRN2", target_bir_lowering=False, num_devices=1)
    aps = {n: nc.dram_tensor(f"{n}_dram", a.shape, F32, kind="ExternalInput").ap() for n, a in arrays.items()}
    out = nc.dram_tensor("out_dram", [TOKENS * STREAMS, W], F32, kind="ExternalOutput").ap()
    build(nc, **aps, out=out)
    r = run_bass_kernel_spmd(nc, [{f"{n}_dram": a for n, a in arrays.items()}], core_ids=[0])
    return r.results[0]["out_dram"].reshape(BATCH, SEQ, D)
```

```python
from contextlib import ExitStack

import concourse.bass as bass
from concourse import mybir

F32 = mybir.dt.float32
ALU = mybir.AluOpType
ACT = mybir.ActivationFunctionType
AX = mybir.AxisListType

P = 128
BATCH, SEQ, D = 2, 2048, 2048
TOKENS = BATCH * SEQ
STREAMS = 4
W = D // STREAMS
KB = W // P
DT = D // P
TPR = P // STREAMS
Q = 4
GT = Q * TPR
G = 8
R = G * Q
BLOCKS = TOKENS // (G * GT)
GH = 2 * G
HALVES = TOKENS // (GH * GT)
RING = 4
S = 16
RANK = 64
NP = RANK + 2 * S
NL = 24
T = 512
CHUNKS = TOKENS // T
CPB = SEQ // T
LN_EPS = 1e-5
RMS_EPS = 1.1920929e-07
TAU_INV = 10.0
ITERS_PER_ABSORB = 7
ABSORBS = 7
ASKS = 6 + 2 * ABSORBS
ABSORB_STEPS = 12 * ITERS_PER_ABSORB - 3
STEPS = 22 + ABSORB_STEPS * ABSORBS
EXP_AND_LN = "natural_log_exp_and_others"
ONE, TWO = 1, 2

C_IDENT = 0
C_HALF = C_IDENT + P
C_SEL = C_HALF + 8
C_STREAM = C_SEL + Q * P
C_TOKEN = C_STREAM + STREAMS
C_COLS = C_TOKEN + TPR


class Memory:

    def __init__(self, nc, ctx, tag):
        self.nc, self.ctx, self.tag = nc, ctx, tag

    def sb(self, name, shape):
        return self.ctx.enter_context(self.nc.sbuf_tensor(f"{self.tag}_{name}", shape, F32))

    def ps(self, name, shape):
        return self.ctx.enter_context(self.nc.psum_tensor(f"{self.tag}_{name}", shape, F32))


def signals(nc, ctx, tag, names, pairs=("stored",)):
    s = {n: ctx.enter_context(nc.semaphore(f"{tag}_{n}")) for n in names}
    for n in pairs:
        s[n] = [ctx.enter_context(nc.semaphore(f"{tag}_{n}{h}")) for h in range(2)]
    return s


class Chain:

    def __init__(self, eng, sem, base):
        self.eng, self.sem, self.base, self.steps = eng, sem, base, 0

    def done(self, ins):
        ins.then_inc(self.sem, 1)
        self.steps += 1

    def wait(self):
        self.eng.wait_ge(self.sem, self.base + self.steps)

    def then(self, ins):
        self.done(ins)
        self.wait()

    def both(self, op):
        for h in range(2):
            self.eng.wait_ge(self.sem, self.base + self.steps - 1)
            self.done(op(h))


def bcast(ap, shape):
    return ap.broadcast_to(shape)


CALLS = BLOCKS + 1


def row_statistics(nc, e, m, s, rows, b, rms, half=None):
    V = nc.vector
    call = half if half is not None else b + 1
    begin, end = (0, G) if half is None else (half * G // 2, (half + 1) * G // 2)
    with e.Fori(begin // 2, end // 2, 1) as gg:
        for h in range(2):
            e.wait_ge(s["loaded"][h], 16 + (b * (G // 2) + gg + 1) * 16)
            for q in range(Q):
                r = (gg * 2 + h) * Q + q
                V.bn_stats(m.bn[:, bass.ds(r, 1), :], rows[:, bass.ds((b % 2) * R + r, 1), :]).then_inc(s["bn"], 1)
    e.wait_ge(s["bn"], b * R + end * Q)
    c = Chain(e, s["stat"], call * (28 if rms else 20))
    c.done(V.tensor_tensor(m.mvc[:, 0, :], m.bn[:, :, 1], m.bn[:, :, 4], ALU.add))
    c.done(V.tensor_tensor(m.dev[:, :], m.bn[:, :, 1], m.bn[:, :, 4], ALU.subtract))
    c.then(V.tensor_tensor(m.dev2[:, :], m.bn[:, :, 2], m.bn[:, :, 5], ALU.add))
    c.then(V.tensor_tensor(m.dev[:, :], m.dev[:, :], m.dev[:, :], ALU.mult))
    c.then(V.scalar_tensor_tensor(m.mvc[:, 1, :], m.dev[:, :], W / 4, m.dev2[:, :], ALU.mult, ALU.add))
    c.done(V.transpose(m.mT[:, 0, :], m.mvc[:, 0, :]))
    c.then(V.transpose(m.mT[:, 1, :], m.mvc[:, 1, :]))
    mT = m.mT[:, 0, :].rearrange("p (t j) -> p t j", j=STREAMS)
    vT = m.mT[:, 1, :].rearrange("p (t j) -> p t j", j=STREAMS)
    dT = m.dT[:, :].rearrange("p (t j) -> p t j", j=STREAMS)
    mean, rstd, shift, ms, std = (m.tok[:, k, :] for k in range(5))
    c.then(V.tensor_reduce(m.sum8[:, :], mT, AX.X, ALU.add))
    c.done(V.tensor_scalar(mean, m.sum8[:, :], 1.0 / (2 * STREAMS), None, ALU.mult))
    c.then(V.tensor_scalar(m.t8[:, :], m.sum8[:, :], 1.0 / STREAMS, None, ALU.mult))
    c.then(V.tensor_tensor(dT, mT, bcast(m.t8[:, :].unsqueeze(2), [P, 8, STREAMS]), ALU.subtract))
    c.then(V.tensor_tensor(dT, dT, dT, ALU.mult))
    c.then(V.scalar_tensor_tensor(dT, dT, W / 4, vT, ALU.mult, ALU.add))
    c.then(V.tensor_reduce(m.var8[:, :], dT, AX.X, ALU.add))
    V.tensor_scalar(m.ve[:, :], m.var8[:, :], 1.0 / D, LN_EPS, ALU.mult, ALU.add).then_inc(s["ve"], 1)
    e.wait_ge(s["pow"], (call * 2 if rms else call) + 1)
    if rms:
        c.then(V.tensor_scalar(m.var8[:, :], m.var8[:, :], 1.0 / D, None, ALU.mult))
        c.then(V.tensor_tensor(m.t8[:, :], m.var8[:, :], m.pow1[:, :], ALU.mult))
        c.then(V.tensor_tensor(m.t8[:, :], m.t8[:, :], m.pow1[:, :], ALU.mult))
        V.tensor_scalar(m.msq[:, :], m.t8[:, :], RMS_EPS, None, ALU.add).then_inc(s["ve"], 1)
        e.wait_ge(s["pow"], call * 2 + 2)
        c.done(V.tensor_tensor(rstd, m.pow1[:, :], m.pow2[:, :], ALU.mult))
        c.then(V.tensor_tensor(ms, m.msq[:, :], m.pow2[:, :], ALU.mult))
        c.then(V.tensor_tensor(m.t8[:, :], m.ve[:, :], m.pow1[:, :], ALU.mult))
        c.then(V.tensor_tensor(std, m.t8[:, :], ms, ALU.mult))
    else:
        c.then(V.tensor_copy(rstd, m.pow1[:, :]))
    c.then(V.scalar_tensor_tensor(shift, mean, -1.0, rstd, ALU.mult, ALU.mult))
    n = 5 if rms else 3
    c.then(V.tensor_copy(m.tokx[:, 0:8 * n, :], bcast(
        m.tok[:, 0:n, :].rearrange("p a t -> p (a t)").unsqueeze(2), [P, 8 * n, STREAMS])))
    for k in range(n):
        ins = V.transpose(m.rowt[:, k, :], m.tokx[:, 8 * k:8 * k + 8, :].rearrange("p t j -> p (t j)"))
        c.then(ins) if k == n - 1 else c.done(ins)
    V.tensor_copy(m.row[:, 0:n, bass.ds(b * R + begin * Q, (end - begin) * Q)],
                  m.rowt[:, 0:n, begin * Q:end * Q]).then_inc(s["row"], 1)
    assert c.steps == (28 if rms else 20), c.steps


def normalise(nc, m, tile, r):
    return nc.scalar.activation(tile, tile, ACT.Identity, scale=m.row[:, 1, bass.ds(r, 1)],
                                bias=m.row[:, 2, bass.ds(r, 1)])


def load_groups(sp, s, rows, src):
    for h in range(2):
        sp.sem_inc(s["loaded"][h], 16)

    def load(n, h):
        sp.wait_ge(s["loaded"][h], (n // 2 + 1) * 16)
        sp.dma_start(rows[:, bass.ds((n % (2 * G)) * Q, Q), :],
                     rows_of(src, n)).then_inc(s["loaded"][h], 16)

    with sp.Fori(0, G, 1) as i:
        for h in range(2):
            load(i * 2 + h, h)
    with sp.Fori(G, BLOCKS * G // 2, 1) as i:
        for h in range(2):
            sp.wait_ge(s["tp_full"], (i * 2 + h - 2 * G + 1) * KB)
            load(i * 2 + h, h)


def rows_of(x, n):
    return x[bass.ts(n, Q * P), :].rearrange("(q p) c -> p q c", p=P)


def statistics_buffers(m):
    m.bn = m.sb("bn", [P, R, 6])
    m.dev = m.sb("dev", [P, R])
    m.dev2 = m.sb("dev2", [P, R])
    m.mvc = m.sb("mvc", [P, 2, R])
    m.mT = m.sb("mT", [P, 2, 32])
    m.dT = m.sb("dT", [P, 32])
    m.sum8, m.var8, m.ve, m.msq, m.pow1, m.pow2, m.t8 = (
        m.sb(n, [P, 8]) for n in ("sum8", "var8", "ve", "msq", "pow1", "pow2", "t8"))
    m.tok = m.sb("tok", [P, 5, 8])
    m.tokx = m.sb("tokx", [P, 40, STREAMS])
    m.rowt = m.sb("rowt", [P, 5, R])
    m.row = m.sb("row", [P, 5, BLOCKS * R])


def first_block_statistics(nc, e, m, s, rows, rms):
    nc.vector.memset(m.bn[:, :, :], 0.0).then_inc(s["zeroed"], 1)
    e.wait_ge(s["zeroed"], 1)
    for half in range(2):
        row_statistics(nc, e, m, s, rows, 0, rms, half)


def pool_roots(nc, e, m, s, call, rms):
    e.wait_ge(s["ve"], (call * 2 if rms else call) + 1)
    nc.gpsimd.tensor_tensor(m.pow1[:, :], m.ve[:, :], m.minus_half, ALU.pow).then_inc(s["pow"], 1)
    if rms:
        e.wait_ge(s["ve"], call * 2 + 2)
        nc.gpsimd.tensor_tensor(m.pow2[:, :], m.msq[:, :], m.minus_half, ALU.pow).then_inc(s["pow"], 1)


def wait_for_row(e, s, n, early):
    e.wait_ge(s["row"], 1 if early else n // G + 2)


def ffn_program(nc, tag, s, src, dst, consts, w_logit, base, gate, w_branch):
    with ExitStack() as ctx:
        m = Memory(nc, ctx, tag)
        V, A, PE, POOL = nc.vector, nc.scalar, nc.tensor, nc.gpsimd
        const = m.sb("const", [P, C_COLS])
        ident = const[:, C_IDENT:C_IDENT + P]
        sel = const[:, C_SEL:C_SEL + Q * P].rearrange("p (q n) -> p q n", q=Q)
        stream_mask = const[:, C_STREAM:C_STREAM + STREAMS]
        token_mask = const[:, C_TOKEN:C_TOKEN + TPR]
        m.minus_half = const[:, C_HALF:C_HALF + 8]
        statistics_buffers(m)
        xh = m.sb("xh", [P, GH * Q, W])
        ring = m.sb("ring", [P, RING * Q, W])
        xT = ring[:, 0:2 * Q, :].rearrange("p (h a) (b t) -> p h (a b) t", h=2, t=GT)
        wl = m.sb("wl", [P, DT, NL])
        wb = m.sb("wb", [P, KB, W])
        base_b = m.sb("base_b", [P, NL])
        gate_b, ge, gs, g_half, i_half = (
            m.sb(n, [P, 1]) for n in ("gate_b", "ge", "gs", "g_half", "i_half"))
        lg = m.sb("lg", [P, HALVES * GH, NL])
        z, pr, tmp = (m.sb(n, [P, GH, 16]) for n in ("z", "pr", "tmp"))
        uv, luv = (m.sb(n, [P, 2, GH, 4]) for n in ("uv", "luv"))
        sm = m.sb("sm", [P, GH, 4])
        hp = m.sb("hp", [P, 2 * GH, 4])
        hpm = m.sb("hpm", [P, 2 * GH])
        h5 = m.sb("h5", [P, GH, 5, 4])
        h_post = m.sb("h_post", [P, HALVES * GH, 4])
        rep = m.sb("rep", [P, GH * 5, 4])
        m5 = m.sb("m5", [P, Q, HALVES * GH, 5])
        dsc = m.sb("dsc", [P, GH * Q])
        dm = m.sb("dm", [P, Q, GH, 4])
        mix_blk = m.sb("mix_blk", [P, 2, Q, TPR, 4])
        pre_blk = m.sb("pre_blk", [P, 2, Q, TPR])
        post_blk = m.sb("post_blk", [P, 2, Q * TPR, 4])
        xpT = m.sb("xpT", [P, KB * GT])
        y_sb = m.sb("y_sb", [P, 2, W])
        lp = m.ps("lp", [P, NL])
        rp = m.ps("rp", [P, GH * 20])
        xp = m.ps("xp", [P, W])
        yp = m.ps("yp", [P, W])
        op = [m.ps(f"op{i}", [P, W]) for i in range(2)]
        tp = [m.ps("tp0", [P, W]), m.ps("tp1", [P, W]), xp, yp]
        block = ctx.enter_context(nc.Block())


        @block.sync
        def _(sp):
            sp.dma_start(const[:, :], consts).then_inc(s["const"], 16)
            sp.dma_start(wl[:, :, :], w_logit).then_inc(s["weights"], 16)
            sp.dma_start(base_b[:, :], base.partition_broadcast(P)).then_inc(s["weights"], 16)
            sp.dma_start(gate_b[:, :], gate.partition_broadcast(P)).then_inc(s["weights"], 16)
            load_groups(sp, s, xh, src)
            sp.dma_start(wb[:, :, :], w_branch).then_inc(s["branch"], 16)

            def load_again(n, h):
                sp.wait_ge(s["again"][h], (n // 2 + 1) * 16)
                sp.dma_start(ring[:, bass.ds((n % RING) * Q, Q), :],
                             rows_of(src, n)).then_inc(s["again"][h], 16)

            for h in range(2):
                sp.sem_inc(s["again"][h], 16)
            sp.wait_ge(s["logits"], TWO + HALVES * GH)
            for n in range(RING):
                load_again(n, n % 2)
            with sp.Fori(RING // 2, GH // 2, 1) as i:
                for h in range(2):
                    sp.wait_ge(s["stored"][h], (i - RING // 2) * 16 + 32)
                    load_again(i * 2 + h, h)

        def slot_rows(n):
            return (ring, (n % RING) * Q) if n < GH else (xh, (n - GH) * Q)

        @block.gpsimd
        def _(pool):
            pool.wait_ge(s["const"], 16)
            with pool.Fori(0, CALLS, 1) as call:
                pool_roots(nc, pool, m, s, call, True)


            def build_pre(n, h, half):
                pool.wait_ge(s["coef"], half + 1)
                pool.wait_ge(s["xp_full"], n + 1)
                POOL.tensor_tensor(
                    pre_blk[:, h, :, :], bcast(token_mask.unsqueeze(1), [P, Q, TPR]),
                    bcast(m5[:, :, bass.ds(n, 1), 4], [P, Q, TPR]), ALU.mult).then_inc(s["pre_blk"], 1)

            def build_mix(n, h):
                pool.wait_ge(s["blk_free"], n + 1)
                for q in range(Q):
                    POOL.tensor_tensor(
                        mix_blk[:, h, q, :, :], bcast(token_mask.unsqueeze(2), [P, TPR, 4]),
                        bcast(m5[:, q, bass.ds(n, 1), 0:4], [P, TPR, 4]),
                        ALU.mult).then_inc(s["mix_blk"], 1)
                POOL.tensor_tensor(
                    post_blk[:, h, :, :], bcast(ident.unsqueeze(2), [P, P, 4]),
                    bcast(h_post[:, bass.ds(n, 1), :], [P, P, 4]), ALU.mult).then_inc(s["post_blk"], 1)

            build_pre(0, 0, 0)
            for half in range(HALVES):
                with pool.Fori(half * GH // 2, (half + 1) * GH // 2 - 1, 1) as i:
                    for h in range(2):
                        build_pre(i * 2 + h + 1, 1 - h, half)
                        build_mix(i * 2 + h, h)
                end = (half + 1) * GH
                build_pre(end - 1, 1, half)
                build_mix(end - 2, 0)
                build_mix(end - 1, 1)
                if half + 1 < HALVES:
                    build_pre(end, 0, half + 1)

        @block.tensor
        def _(pe):
            pe.wait_ge(s["const"], 16)
            pe.wait_ge(s["weights"], 48)
            pe.sem_inc(s["logits"], TWO)
            pe.sem_inc(s["xp_full"], TWO)
            pe.sem_inc(s["y_full"], ONE)

            def logits(half):
                for g in range(GH + 1):
                    n = half * GH + g
                    if g < GH:
                        pe.wait_ge(s["norm"], n * Q + Q)
                        for k in range(KB):
                            pe.wait_ge(s["xT_in"], n * KB + k + 1)
                            for q in range(Q):
                                mm = PE.transpose(tp[k][:, q * P:(q + 1) * P],
                                                  xh[:, g * Q + q, k * P:(k + 1) * P], ident)
                            mm.then_inc(s["tp_full"], 1)
                    if g >= 1:
                        pe.wait_ge(s["xT_in"], KB + n * KB)
                        pe.wait_ge(s["lg_in"], n)
                        for d in range(DT):
                            mm = PE.matmul(lp[:, :], xT[:, (g - 1) % 2, d, :], wl[:, d, :],
                                           start=(d == 0), stop=(d == DT - 1))
                        mm.then_inc(s["logits"], 1)

            def coefficients_to_rows(half):
                pe.wait_ge(s["h5"], half + 1)
                for q in range(Q):
                    pe.wait_ge(s["rp_free"], half * Q + q + 1)
                    PE.matmul(rp[:, :], sel[:, q, :], h5[:, :, :, :].rearrange("p g i j -> p (g i j)"),
                              start=True, stop=True).then_inc(s["rp_full"], 1)

            def mix(half):
                def pre_mix(n):
                    rows, r = slot_rows(n)
                    if half == 0:
                        pe.wait_ge(s["norm_again"], n * Q + Q)
                    pe.wait_ge(s["pre_blk"], n + 1)
                    pe.wait_ge(s["xpT_in"], n + 1)
                    for k in range(KB):
                        for q in range(Q):
                            mm = PE.matmul(xp[:, k * GT + q * TPR:k * GT + (q + 1) * TPR],
                                           rows[:, r + q, k * P:(k + 1) * P], pre_blk[:, n % 2, q, :],
                                           start=True, stop=True)
                    mm.then_inc(s["xp_full"], 1)

                def branch(n):
                    pe.wait_ge(s["xpT_in"], ONE + n + 1)
                    pe.wait_ge(s["y_in"], n + 1)
                    for k in range(KB):
                        mm = PE.matmul(yp[:, :], xpT[:, k * GT:(k + 1) * GT], wb[:, k, :],
                                       start=(k == 0), stop=(k == KB - 1))
                    mm.then_inc(s["y_full"], 1)

                def mix_rows(n, q):
                    rows, r = slot_rows(n)
                    if q == 0:
                        pe.wait_ge(s["mix_blk"], n * Q + Q)
                        pe.wait_ge(s["post_blk"], n + 1)
                        pe.wait_ge(s["y_in"], ONE + n + 1)
                    pe.wait_ge(s["o_out"], n * Q + q + 1)
                    PE.matmul(op[q % 2][:, :], mix_blk[:, n % 2, q, :, :].rearrange("p t i -> p (t i)"),
                              rows[:, r + q, :], start=True, stop=False)
                    PE.matmul(op[q % 2][:, :], post_blk[:, n % 2, q * TPR:(q + 1) * TPR, :]
                              .rearrange("p t i -> p (t i)"), y_sb[:, n % 2, :],
                              start=False, stop=True).then_inc(s["o_full"], 1)

                begin, end = half * GH, (half + 1) * GH
                pre_mix(begin)
                branch(begin)
                for n in range(begin, end):
                    if n + 1 < end:
                        pre_mix(n + 1)
                    mix_rows(n, 0)
                    mix_rows(n, 1)
                    if n + 1 < end:
                        branch(n + 1)
                    mix_rows(n, 2)
                    mix_rows(n, 3)

            for half in range(HALVES):
                logits(half)
            pe.wait_ge(s["branch"], 16)
            for half in range(HALVES):
                coefficients_to_rows(half)
                mix(half)

        @block.scalar
        def _(act):
            act.preload_act_table_set(EXP_AND_LN)
            act.wait_ge(s["weights"], 48)
            A.activation(ge[:, :], gate_b[:, :], ACT.Exp, scale=-1.0).then_inc(s["gate"], 1)
            act.sem_inc(s["xT_in"], KB)
            act.sem_inc(s["lg_in"], ONE)
            act.sem_inc(s["xpT_in"], ONE)
            act.sem_inc(s["y_in"], ONE)
            act.sem_inc(s["o_out"], TWO)
            act.sem_inc(s["blk_free"], TWO)
            act.sem_inc(s["stored"][0], 16)
            act.sem_inc(s["stored"][1], 16)

            def transposed(n, h):
                act.wait_ge(s["logits"], n + 1)
                for k in range(KB):
                    act.wait_ge(s["tp_full"], n * KB + k + 1)
                    A.activation(xT[:, h, k::KB, :],
                                 tp[k][:, :].rearrange("p (n j) -> p j n", j=STREAMS),
                                 ACT.Copy).then_inc(s["xT_in"], 1)

            def logits_in(n):
                act.wait_ge(s["logits"], TWO + n + 1)
                A.activation(lg[:, bass.ds(n, 1), :], lp[:, :].unsqueeze(1), ACT.Copy).then_inc(s["lg_in"], 1)

            def normalise_group(n, early=False):
                wait_for_row(act, s, n, early)
                for q in range(Q):
                    normalise(nc, m, xh[:, bass.ds((n % GH) * Q + q, 1), :], n * Q + q).then_inc(s["norm"], 1)

            def pair(n, first=False, begin=False, end=False):
                early = begin and first and n == 0
                if begin:
                    normalise_group(n, early)
                    normalise_group(n + 1, early)
                if not end:
                    normalise_group(n + 2, early)
                transposed(n, 0)
                if not first:
                    logits_in(n - 1)
                if not end:
                    normalise_group(n + 3, early)
                transposed(n + 1, 1)
                logits_in(n)

            def normalise_again(n, h, q):
                act.wait_ge(s["again"][h], 16 + (n // 2 + 1) * 16)
                normalise(nc, m, ring[:, bass.ds((n % RING) * Q + q, 1), :],
                          n * Q + q).then_inc(s["norm_again"], 1)

            def softmax_functions(half):
                for i, (out, in_, f) in enumerate(
                        [(hp[:, :, :], hp[:, :, :], ACT.Exp)]
                        + [(tmp[:, :, :], z[:, :, :], ACT.Exp), (sm[:, :, :], sm[:, :, :], ACT.Ln)] * 2
                        + [(pr[:, :, :], z[:, :, :], ACT.Exp)]):
                    act.wait_ge(s["ask"], half * ASKS + i + 1)
                    A.activation(out, in_, f).then_inc(s["given"], 1)

            def absorb_functions(half, a):
                act.wait_ge(s["ask"], half * ASKS + 6 + a * 2 + 1)
                A.activation(luv[:, :, :, :], uv[:, :, :, :], ACT.Ln).then_inc(s["given"], 1)
                act.wait_ge(s["ask"], half * ASKS + 6 + a * 2 + 2)
                A.activation(pr[:, :, :], z[:, :, :], ACT.Exp).then_inc(s["given"], 1)

            def pre_mixed(n):
                act.wait_ge(s["xp_full"], TWO + n + 1)
                act.wait_ge(s["y_full"], n + 1)
                A.activation(xpT[:, :], xp[:, :], ACT.Copy).then_inc(s["xpT_in"], 1)

            def branched(n, h):
                act.wait_ge(s["y_full"], ONE + n + 1)
                A.activation(y_sb[:, h, :], yp[:, :], ACT.Copy).then_inc(s["y_in"], 1)

            def mixed(n, h, half, last=False, ahead=True):
                rows, r = (ring, (n % RING) * Q) if half == 0 else (xh, (n - GH) * Q)
                if not last:
                    pre_mixed(n + 1)
                for q in range(Q):
                    if q == 2 and not last:
                        branched(n + 1, 1 - h)
                    act.wait_ge(s["o_full"], n * Q + q + 1)
                    A.activation(rows[:, bass.ds(r + q, 1), :], op[q % 2][:, :].unsqueeze(1), ACT.Identity,
                                 bias=m.row[:, 0, bass.ds(n * Q + q, 1)]).then_inc(s["o_out"], 1)
                    if q < 2 and half == 0 and ahead:
                        normalise_again(n + 2, h, 2 * q)
                        normalise_again(n + 2, h, 2 * q + 1)
                act.sem_inc(s["blk_free"], 1)
                act.wait_ge(s["o_out"], TWO + n * Q + Q)
                act.wait_ge(s["stored"][h], (n // 2 + 1) * 16)
                act.dma_start(rows_of(dst, n), rows[:, bass.ds(r, Q), :]).then_inc(s["stored"][h], 16)

            for b in range(BLOCKS // 2):
                pair(b * G, first=(b == 0), begin=True)
                with act.Fori(b * G // 2 + 1, (b + 1) * G // 2 - 1, 1) as i:
                    pair(i * 2)
                pair((b + 1) * G - 2, end=True)
            logits_in(GH - 1)
            softmax_functions(0)
            folding_after = (0, 1, 3, 4, 5, 6)
            for i in range(GH // 2):
                pair(GH + i * 2, first=(i == 0), begin=(i % (G // 2) == 0), end=(i % (G // 2) == G // 2 - 1))
                if i in folding_after:
                    absorb_functions(0, folding_after.index(i))
                if i == GH // 2 - 1:
                    logits_in(2 * GH - 1)
            absorb_functions(0, ABSORBS - 1)
            for n in range(2):
                for q in range(Q):
                    normalise_again(n, n, q)
            pre_mixed(0)
            branched(0, 0)
            softmax_functions(1)
            mixed(0, 0, 0)
            mixed(1, 1, 0)
            absorb_functions(1, 0)
            with act.Fori(1, ABSORBS, 1) as a:
                for h in range(2):
                    mixed(a * 2 + h, h, 0)
                absorb_functions(1, a)
            mixed(GH - 2, 0, 0, ahead=False)
            mixed(GH - 1, 1, 0, last=True, ahead=False)
            pre_mixed(GH)
            branched(GH, 0)
            with act.Fori(GH // 2, GH - 1, 1) as i:
                for h in range(2):
                    mixed(i * 2 + h, h, 1)
            mixed(2 * GH - 2, 0, 1)
            mixed(2 * GH - 1, 1, 1, last=True)
            for h in range(2):
                act.wait_ge(s["stored"][h], 16 + 16 * GH)

        @block.vector
        def _(dve):
            dve.wait_ge(s["weights"], 48)
            dve.wait_ge(s["const"], 16)
            dve.sem_inc(s["rp_free"], ONE)
            c0 = Chain(dve, s["setup"], 0)
            dve.wait_ge(s["gate"], 1)
            c0.then(V.tensor_scalar(gs[:, :], ge[:, :], 1.0, None, ALU.add))
            c0.then(V.reciprocal(ge[:, :], gs[:, :]))
            c0.then(V.tensor_scalar(g_half[:, :], ge[:, :], 0.5, None, ALU.mult))
            c0.then(V.tensor_scalar(i_half[:, :], ge[:, :], -0.5, 0.5, ALU.mult, ALU.add))
            g4, g4_part = [P, GH, 4, 4], [P, GH // 2, 4, 4]

            def part(h):
                return slice(h * GH // 2, (h + 1) * GH // 2)

            def by_row(t):
                return t[:, :, :].rearrange("p g (i j) -> p g i j", i=4)

            def by_col(t):
                return t[:, :, :].rearrange("p g (i j) -> p g j i", i=4)

            def over(v):
                return bcast(v.unsqueeze(3), g4)

            def weights_of(half):
                groups = slice(half * GH, (half + 1) * GH)
                c = Chain(dve, s["sink"], half * STEPS)
                asked = 0

                def ask(ins):
                    nonlocal asked
                    ins.then_inc(s["ask"], 1)
                    asked += 1
                    dve.wait_ge(s["given"], half * ASKS + asked)

                dve.wait_ge(s["lg_in"], ONE + (half + 1) * GH)
                lh = lg[:, groups, :]
                c.then(V.tensor_tensor(lh, lh, bcast(base_b[:, :].unsqueeze(1), [P, GH, NL]), ALU.add))
                pp = lg[:, groups, 16:24].rearrange("p g (s n) -> p g s n", s=2)
                hv = hp[:, :, :].rearrange("p (g s) n -> p g s n", s=2)
                c.then(V.tensor_reduce(hpm[:, :], pp, AX.X, ALU.max))
                ask(V.tensor_tensor(hv, pp, bcast(hpm[:, :].rearrange("p (g s) -> p g s", s=2)
                                                  .unsqueeze(3), [P, GH, 2, 4]), ALU.subtract))
                c.then(V.tensor_reduce(hpm[:, :], hp[:, :, :], AX.X, ALU.add))
                c.then(V.reciprocal(hpm[:, :], hpm[:, :]))
                c.then(V.tensor_tensor(hp[:, :, :], hp[:, :, :],
                                       bcast(hpm[:, :].unsqueeze(2), [P, 2 * GH, 4]), ALU.mult))
                c.then(V.tensor_scalar(z[:, :, :], lg[:, groups, 0:16], TAU_INV, None, ALU.mult))
                for view in (by_row, by_col):
                    c.then(V.tensor_reduce(sm[:, :, :], view(z), AX.X, ALU.max))
                    ask(V.tensor_tensor(view(z), view(z), over(sm[:, :, :]), ALU.subtract))
                    ask(V.tensor_reduce(sm[:, :, :], view(tmp), AX.X, ALU.add))
                    ins = V.tensor_tensor(view(z), view(z), over(sm[:, :, :]), ALU.subtract)
                    if view is by_row:
                        c.then(ins)
                ins.then_inc(s["ask"], 1)
                first = c.steps

                def absorb(a):
                    dve.wait_ge(s["given"], half * ASKS + 6 + a * 2)
                    ca = Chain(dve, s["sink"], half * STEPS + first + a * ABSORB_STEPS)
                    for i in range(ITERS_PER_ABSORB):
                        if i:
                            ca.both(lambda h: V.tensor_tensor(
                                by_row(tmp)[:, part(h)], by_row(pr)[:, part(h)],
                                bcast(uv[:, 1, part(h), :].unsqueeze(2), g4_part), ALU.mult))
                        ca.both(lambda h: V.tensor_reduce(sm[:, part(h), :], by_row(tmp if i else pr)[:, part(h)],
                                                          AX.X, ALU.add))
                        ca.both(lambda h: V.reciprocal(uv[:, 0, part(h), :], sm[:, part(h), :]))
                        ca.both(lambda h: V.tensor_tensor(
                            by_row(tmp)[:, part(h)], by_row(pr)[:, part(h)],
                            bcast(uv[:, 0, part(h), :].unsqueeze(3), g4_part), ALU.mult))
                        ca.both(lambda h: V.tensor_reduce(sm[:, part(h), :], by_col(tmp)[:, part(h)],
                                                          AX.X, ALU.add))
                        if i < ITERS_PER_ABSORB - 1:
                            ca.both(lambda h: V.reciprocal(uv[:, 1, part(h), :], sm[:, part(h), :]))
                    ca.wait()
                    V.reciprocal(uv[:, 1, :, :], sm[:, :, :]).then_inc(s["ask"], 1)
                    dve.wait_ge(s["given"], half * ASKS + 6 + a * 2 + 1)
                    ca.then(V.tensor_tensor(by_row(z), by_row(z), over(luv[:, 0, :, :]), ALU.add))
                    V.tensor_tensor(by_row(z), by_row(z), bcast(luv[:, 1, :, :].unsqueeze(2), g4),
                                    ALU.add).then_inc(s["ask"], 1)
                    assert ca.steps == ABSORB_STEPS, ca.steps

                if half == 0:
                    with dve.Fori(0, 2, 1) as a:
                        absorb(a)
                    row_statistics(nc, dve, m, s, xh, BLOCKS - 1, True)
                    with dve.Fori(2, ABSORBS, 1) as a:
                        absorb(a)
                else:
                    with dve.Fori(0, ABSORBS, 1) as a:
                        absorb(a)
                c.steps += ABSORB_STEPS * ABSORBS
                dve.wait_ge(s["given"], half * ASKS + ASKS)
                c.done(V.tensor_copy(h5[:, :, 4, :], hv[:, :, 0, :]))
                c.done(V.tensor_scalar(h_post[:, groups, :], hv[:, :, 1, :], 0.5, None, ALU.mult))
                V.tensor_scalar(h5[:, :, 0:4, :].rearrange("p g i j -> p g (i j)"), pr[:, :, :],
                                g_half[:, 0:1], None, ALU.mult).then_inc(s["h5"], 1)
                for q in range(Q):
                    dve.wait_ge(s["rp_full"], half * Q + q + 1)
                    c.then(V.tensor_tensor(rep[:, :, :], rp[:, :].rearrange("p (n j) -> p n j", j=4),
                                           bcast(stream_mask.unsqueeze(1), [P, GH * 5, 4]), ALU.mult))
                    dve.sem_inc(s["rp_free"], 1)
                    c.then(V.tensor_reduce(m5[:, q, groups, :].rearrange("p g i -> p (g i)"),
                                           rep[:, :, :], AX.X, ALU.add))
                mh = m5[:, :, groups, :]
                ms = m.row[:, 3, half * GH * Q:(half + 1) * GH * Q]
                std = m.row[:, 4, half * GH * Q:(half + 1) * GH * Q]
                c.then(V.tensor_tensor(mh, mh, bcast(
                    ms.rearrange("p (g q) -> p q g", q=Q).unsqueeze(3), [P, Q, GH, 5]), ALU.mult))
                c.then(V.scalar_tensor_tensor(dsc[:, :], ms, i_half[:, 0:1], std, ALU.mult, ALU.add))
                c.then(V.tensor_tensor(dm[:, :, :, :],
                                       bcast(dsc[:, :].rearrange("p (g q) -> p q g", q=Q).unsqueeze(3), [P, Q, GH, 4]),
                                       bcast(stream_mask.unsqueeze(1).unsqueeze(1), [P, Q, GH, 4]), ALU.mult))
                mx = m5[:, :, groups, 0:4]
                V.tensor_tensor(mx, mx, dm[:, :, :, :], ALU.add).then_inc(s["coef"], 1)
                assert asked == 5 and c.steps == STEPS, (asked, c.steps)

            first_block_statistics(nc, dve, m, s, xh, True)
            with dve.Fori(1, BLOCKS - 1, 1) as b:
                row_statistics(nc, dve, m, s, xh, b, True)
            for half in range(HALVES):
                weights_of(half)


FFN_SIGNALS = ["const", "weights", "branch", "coef", "blk_free", "pre_blk", "mix_blk", "post_blk", "norm", "norm_again",
               "tp_full", "xT_in", "logits", "lg_in", "h5", "rp_free", "rp_full", "xp_full", "xpT_in",
               "y_full", "y_in", "o_full", "o_out", "gate", "ask", "given", "setup", "sink",
               "zeroed", "bn", "stat", "ve", "pow", "row"]


def project_program(nc, tag, s, src, normed, projected, consts, w_proj):
    with ExitStack() as ctx:
        m = Memory(nc, ctx, tag)
        V, A, PE = nc.vector, nc.scalar, nc.tensor
        const = m.sb("const", [P, C_SEL])
        ident = const[:, C_IDENT:C_IDENT + P]
        m.minus_half = const[:, C_HALF:C_HALF + 8]
        statistics_buffers(m)
        xh = m.sb("xh", [P, 2 * R, W])
        wp = m.sb("wp", [P, DT, NP])
        CG = T // GT
        xT = m.sb("xT", [P, DT, 2, T])
        proj = m.sb("proj", [NP, T])
        tp = [m.ps(f"tp{i}", [P, W]) for i in range(4)]
        pp = [m.ps(f"pp{i}", [NP, T]) for i in range(2)]
        block = ctx.enter_context(nc.Block())
        FOUR = len(tp)

        @block.sync
        def _(sp):
            sp.dma_start(const[:, :], consts[:, 0:C_SEL]).then_inc(s["const"], 16)
            sp.dma_start(wp[:, :, :], w_proj).then_inc(s["weights"], 16)
            load_groups(sp, s, xh, src)

        @block.gpsimd
        def _(pool):
            pool.wait_ge(s["const"], 16)
            with pool.Fori(0, CALLS, 1) as call:
                pool_roots(nc, pool, m, s, call, False)

        @block.vector
        def _(dve):
            dve.wait_ge(s["const"], 16)
            first_block_statistics(nc, dve, m, s, xh, False)
            with dve.Fori(1, BLOCKS, 1) as b:
                row_statistics(nc, dve, m, s, xh, b, False)


        @block.tensor
        def _(pe):
            pe.wait_ge(s["const"], 16)
            pe.wait_ge(s["weights"], 16)

            def project_part(c, part):
                if part == 0:
                    pe.wait_ge(s["xT_in"], FOUR + (c + 1) * CG * KB)
                    pe.wait_ge(s["proj_in"], c + 1)
                for d in range(part * DT // CG, (part + 1) * DT // CG):
                    mm = PE.matmul(pp[c % 2][:, :], wp[:, d, :], xT[:, d, c % 2, :],
                                   start=(d == 0), stop=(d == DT - 1))
                if part == CG - 1:
                    mm.then_inc(s["proj_full"], 1)

            for b in range(BLOCKS):
                for g in range(G):
                    n = b * G + g
                    pe.wait_ge(s["norm"], n * Q + Q)
                    for k in range(KB):
                        pe.wait_ge(s["xT_in"], n * KB + k + 1)
                        for q in range(Q):
                            mm = PE.transpose(tp[k][:, q * P:(q + 1) * P],
                                              xh[:, (b % 2) * R + g * Q + q, k * P:(k + 1) * P], ident)
                        mm.then_inc(s["tp_full"], 1)
                    if n >= CG:
                        project_part(n // CG - 1, g % CG)
            for part in range(CG):
                project_part(CHUNKS - 1, part)

        @block.scalar
        def _(act):
            act.sem_inc(s["xT_in"], FOUR)
            act.sem_inc(s["proj_in"], TWO)
            act.sem_inc(s["stored"][0], 16)
            act.sem_inc(s["stored"][1], 16)
            act.sem_inc(s["sent"], 16)

            def normalise_group(n, early=False):
                wait_for_row(act, s, n, early)
                for q in range(Q):
                    normalise(nc, m, xh[:, bass.ds((n % (2 * G)) * Q + q, 1), :],
                              n * Q + q).then_inc(s["norm"], 1)

            def projected_chunk(c, h):
                act.wait_ge(s["proj_full"], c + 1)
                act.wait_ge(s["sent"], (c + 1) * 16)
                A.activation(proj[:, :], pp[h][:, :], ACT.Copy).then_inc(s["proj_in"], 1)
                act.wait_ge(s["proj_in"], TWO + c + 1)
                act.dma_start(projected[:, bass.ts(c, T)], proj[:, :]).then_inc(s["sent"], 16)

            def block_of_chunks(b, first=False):
                normalise_group(b * G, first)
                normalise_group(b * G + 1, first)
                for h in range(2):
                    c = b * 2 + h
                    for g in range(CG):
                        n = c * CG + g
                        if h * CG + g + 2 < G:
                            normalise_group(n + 2, first and n + 2 < G // 2)
                        for k in range(KB):
                            act.wait_ge(s["tp_full"], n * KB + k + 1)
                            if g == 0 and k == 0:
                                if not first:
                                    projected_chunk(c - 2, h)
                                act.wait_ge(s["stored"][h], (b + 1) * 16)
                            A.activation(xT[:, k::KB, h, g * GT:(g + 1) * GT],
                                         tp[k][:, :].rearrange("p (n j) -> p j n", j=STREAMS),
                                         ACT.Copy).then_inc(s["xT_in"], 1)
                    act.wait_ge(s["xT_in"], FOUR + (c + 1) * CG * KB)
                    act.dma_start(normed[bass.ts(c, DT * P), :].rearrange("(d p) t -> p d t", p=P),
                                  xT[:, :, h, :]).then_inc(s["stored"][h], 16)

            block_of_chunks(0, first=True)
            with act.Fori(1, BLOCKS, 1) as b:
                block_of_chunks(b)
            projected_chunk(CHUNKS - 2, 0)
            projected_chunk(CHUNKS - 1, 1)
            for h in range(2):
                act.wait_ge(s["stored"][h], 16 + 16 * BLOCKS)
            act.wait_ge(s["sent"], 16 + 16 * CHUNKS)


PROJECT_SIGNALS = ["const", "weights", "norm", "tp_full", "xT_in", "proj_full", "proj_in", "sent",
                   "zeroed", "bn", "stat", "ve", "pow", "row"]

C_CHAN = S + 2
PE_STATES = (5, 10, 15)
DVE_STATES = tuple(n for n in range(S) if n not in PE_STATES)
NPE, NDVE = len(PE_STATES), len(DVE_STATES)
HSLOTS = 8
GSLOTS = 4
ASLOTS = 3
SCAN_CREDIT = 4
PIECE = 2 * S // (DT // 2)
B_LOADS = 16 * (S // PIECE)
C_LOADS = 16 * (1 + S // PIECE)
K = CHUNKS * DT


def scan_program(nc, tag, s, x_in, normed, projected, x_out, consts, channels, w_dt, keep):
    with ExitStack() as ctx:
        m = Memory(nc, ctx, tag)
        V, A, PE, POOL = nc.vector, nc.scalar, nc.tensor, nc.gpsimd
        ident = m.sb("ident", [P, P])
        keep_sb = m.sb("keep", [P, K])
        bc = m.sb("bc", [P, 2, 2 * S, T])
        dt_in = m.sb("dt_in", [RANK, 2, T])
        xn = m.sb("xn", [P, 2, T])
        x_blk = m.sb("x_blk", [P, 2, T // P, P])
        chan = m.sb("chan", [P, 2, C_CHAN])
        wdt = m.sb("wdt", [RANK, 2, P])
        neg_a = m.sb("neg_a", [P, 2, S])
        rl, ln1p = (m.sb(n, [P, T]) for n in ("rl", "ln1p"))
        neg_dt = m.sb("neg_dt", [P, 2, T])
        diag_d = m.sb("diag_d", [P, 2, P])
        h_last = m.sb("h_last", [P, DT, S])
        h_first = m.sb("h_first", [P, 2, S])
        bx = m.sb("bx", [P, ASLOTS, T])
        hs = m.sb("hs", [P, HSLOTS, T])
        ch = m.sb("ch", [P, GSLOTS, T])
        y_sb = m.sb("y_sb", [P, T])
        o_sb = m.sb("o_sb", [P, 2, T // P, P])
        decay_sb = m.sb("decay_sb", [P, T])
        u_sb = m.sb("u_sb", [P, T])
        u_time = m.sb("u_time", [P, T // P, P])
        b_diag = m.sb("b_diag", [P, 2, NPE, T // P, P])
        decay = [m.ps(f"decay{i}", [P, T]) for i in range(ASLOTS)]
        u = m.ps("u", [P, T])
        acc = [m.ps(f"acc{i}", [P, T]) for i in range(2)]
        bx_pe = m.ps("bx_pe", [P, T])
        dt_raw = turned = turned_u = m.ps("work", [P, T])
        block = ctx.enter_context(nc.Block())
        x_tok = x_in.rearrange("(n j) c -> n (j c)", j=STREAMS)
        out_tok = x_out.rearrange("(n j) c -> n (j c)", j=STREAMS)

        def token_block(x, k):
            return x[bass.ds((k // DT) * T, T), bass.ds((k % DT) * P, P)].rearrange("(a p) c -> p a c", p=P)

        def ring_slot(n):
            return DVE_STATES.index(n) % ASLOTS

        def slot_used(k, n):
            i = DVE_STATES.index(n)
            last = DVE_STATES[i - ASLOTS] if i >= ASLOTS else max(
                v for v in DVE_STATES if ring_slot(v) == i) - S
            return SCAN_CREDIT + k * S + last + 1

        def pe_used(k, n):
            j = PE_STATES.index(n)
            return SCAN_CREDIT + k * S + (PE_STATES[j - 1] if j else PE_STATES[-1] - S) + 1


        def load_states(e, c, i, signal):
            e.dma_start(bc[:, bass.ds(c % 2, 1), bass.ds(i * PIECE, PIECE), :],
                         projected[bass.ds(RANK + i * PIECE, PIECE), bass.ts(c, T)]
                         .unsqueeze(0).unsqueeze(0).partition_broadcast(P)).then_inc(signal, 16)

        @block.sync
        def _(sp):
            def load(k, h):
                sp.wait_ge(s["diag"], k + 1)
                sp.dma_start(chan[:, h, :], channels[bass.ts(k % DT, P), :]).then_inc(s["params"][h], 16)
                sp.dma_start(wdt[:, h, :], w_dt[bass.ts(k % DT, RANK), :]).then_inc(s["params"][h], 16)
                sp.wait_ge(s["skip"], k + 1)
                sp.dma_start(xn[:, h, :], normed[bass.ts(k, P), :]).then_inc(s["xn"][h], 16)
                sp.wait_ge(s["turned"], k + 1)
                sp.dma_start(x_blk[:, h, :, :], token_block(x_tok, k)).then_inc(s["x_blk"][h], 16)

            def load_dt_in(c):
                sp.dma_start(dt_in[:, bass.ds(c % 2, 1), :],
                             projected[0:RANK, bass.ts(c, T)].unsqueeze(1)).then_inc(s["chunk"], 16)

            sp.dma_start(ident[:, :], consts[:, C_IDENT:C_IDENT + P]).then_inc(s["const"], 16)
            sp.dma_start(keep_sb[:, :], keep).then_inc(s["const"], 16)
            load_dt_in(0)
            with sp.Fori(0, CHUNKS - 1, 1) as c:
                for h in range(2):
                    load(c * DT + h, h)
                sp.wait_ge(s["b"], (c + 1) * B_LOADS)
                sp.wait_ge(s["chunk"], c * C_LOADS + C_LOADS)
                sp.wait_ge(s["scaled"], HSLOTS + c * DT * S)
                load_dt_in(c + 1)
                load_states(sp, c + 1, 0, s["b"])
                for first, signal in ((1, s["b"]), (DT // 4, s["chunk"])):
                    with sp.Fori(first, DT // 4 * (1 if first == 1 else 2), 1) as i:
                        for h in range(2):
                            load(c * DT + i * 2 + h, h)
                        load_states(sp, c + 1, i, signal)
            with sp.Fori(0, DT // 2, 1) as i:
                for h in range(2):
                    load((CHUNKS - 1) * DT + i * 2 + h, h)

        @block.scalar
        def _(act):
            act.preload_act_table_set(EXP_AND_LN)
            act.sem_inc(s["diag"], TWO)
            act.sem_inc(s["y_in"], ONE)
            act.sem_inc(s["u_in"], ONE)
            act.sem_inc(s["stored"][0], 16)
            act.sem_inc(s["stored"][1], 16)

            for i in range(DT // 2):
                load_states(act, 0, i, s["b"] if i < DT // 4 else s["chunk"])

            def softplus_abs(k, h):
                act.wait_ge(s["params"][h], (k // 2) * 32 + 32)
                A.activation(neg_a[:, h, :], chan[:, h, 0:S], ACT.Exp).then_inc(s["neg_a"], 1)
                act.wait_ge(s["dt_raw"], k + 1)
                act.wait_ge(s["neg_dt"], k + 1)
                A.activation(ln1p[:, :], dt_raw[:, :], ACT.Abs, bias=chan[:, h, S + 1:S + 2]).then_inc(s["soft"], 1)

            def softplus_relu(k, h):
                A.activation(rl[:, :], dt_raw[:, :], ACT.Relu, bias=chan[:, h, S + 1:S + 2]).then_inc(s["dt_read"], 1)

            def softplus_exp(k):
                act.wait_ge(s["soft"], k * 3 + 1)
                A.activation(ln1p[:, :], ln1p[:, :], ACT.Exp, scale=-1.0).then_inc(s["soft"], 1)

            def softplus_log(k):
                act.wait_ge(s["soft"], k * 3 + 2)
                A.activation(ln1p[:, :], ln1p[:, :], ACT.Ln, bias=1.0).then_inc(s["soft"], 1)

            def make_diag(k, h):
                act.wait_ge(s["skip"], k + 1)
                A.activation(diag_d[:, h, :], ident[:, :], ACT.Copy, scale=chan[:, h, S:S + 1]).then_inc(s["diag"], 1)

            def make_first(k, h, saved):
                act.wait_ge(s["state"], saved)
                A.activation(h_first[:, h, :], h_last[:, bass.ds(k % DT, 1), :].rearrange("p a n -> p (a n)"),
                             ACT.Copy, scale=keep_sb[:, bass.ds(k, 1)]).then_inc(s["first"], 1)

            def copy_u(k):
                act.wait_ge(s["u"], k + 1)
                act.wait_ge(s["u_turned"], k + 1)
                A.activation(u_sb[:, :], u[:, :], ACT.Copy).then_inc(s["u_in"], 1)

            def copy_turned_u(k):
                act.wait_ge(s["u_turned"], ONE + k + 1)
                act.wait_ge(s["bx_pe"], ONE + k * NPE)
                A.activation(u_time[:, :, :].rearrange("p a c -> p (a c)"), turned_u[:, :],
                             ACT.Copy).then_inc(s["u_time"], 1)

            def step(k, h, first=False, last=False):
                act.wait_ge(s["neg_a"], k + 1)
                act.wait_ge(s["neg_dt"], ONE + k + 1)
                for n in range(S):
                    if n in PE_STATES:
                        act.wait_ge(s["scan"], pe_used(k, n))
                        out = decay_sb
                    else:
                        act.wait_ge(s["scan"], slot_used(k, n))
                        out = decay[ring_slot(n)]
                    A.activation(out[:, :], neg_dt[:, h, :], ACT.Exp,
                                 scale=neg_a[:, h, n:n + 1]).then_inc(s["decay"], 1)
                    if n == 3:
                        copy_turned_u(k)
                    if n == 6 and not first:
                        copy_sum(k - 1, 1 - h)
                    if n == 8 and not last:
                        softplus_abs(k + 1, 1 - h)
                    if n == 9 and not last:
                        softplus_relu(k + 1, 1 - h)
                    if n == 10 and not last:
                        softplus_exp(k + 1)
                    if n == 11 and not last:
                        softplus_log(k + 1)
                    if n == 12 and not last:
                        make_diag(k + 1, 1 - h)
                    if n == 13 and not first:
                        copy_turned(k - 1, 1 - h)
                    if n == 14 and not last:
                        make_first(k + 1, 1 - h, k * 2 + 1)
                    if n == S - 1 and not last:
                        copy_u(k + 1)

            def copy_sum(k, h):
                act.wait_ge(s["summed"], GSLOTS + (k + 1) * S)
                act.wait_ge(s["turned"], TWO + k)
                A.activation(y_sb[:, :], acc[h][:, :], ACT.Copy).then_inc(s["y_in"], 1)

            def copy_turned(k, h):
                act.wait_ge(s["turned"], TWO + k + 1)
                act.wait_ge(s["stored"][h], (k // 2) * 16 + 16)
                A.activation(o_sb[:, h, :, :].rearrange("p a c -> p (a c)"), turned[:, :],
                             ACT.Copy).then_inc(s["turned_in"], 1)
                act.wait_ge(s["turned_in"], k + 1)
                act.dma_start(token_block(out_tok, k), o_sb[:, h, :, :]).then_inc(s["stored"][h], 16)

            softplus_abs(0, 0)
            softplus_relu(0, 0)
            softplus_exp(0)
            softplus_log(0)
            act.wait_ge(s["const"], 32)
            make_diag(0, 0)
            make_first(0, 0, 1)
            copy_u(0)
            step(0, 0, first=True)
            with act.Fori(0, (K - 2) // 2, 1) as i:
                step(i * 2 + 1, 1)
                step(i * 2 + 2, 0)
            step(K - 1, 1, last=True)
            copy_sum(K - 1, 1)
            copy_turned(K - 1, 1)
            for h in range(2):
                act.wait_ge(s["stored"][h], 16 + 16 * K // 2)

        @block.vector
        def _(dve):
            dve.memset(h_last[:, :, :], 0.0).then_inc(s["state"], 1)
            dve.sem_inc(s["scan"], SCAN_CREDIT)
            dve.sem_inc(s["neg_dt"], ONE)
            dve.sem_inc(s["bx"], ONE)

            def make_neg_dt(k, h):
                dve.wait_ge(s["soft"], k * 3 + 3)
                dve.wait_ge(s["dt_read"], k + 1)
                V.scalar_tensor_tensor(neg_dt[:, h, :], rl[:, :], -1.0, ln1p[:, :],
                                       ALU.mult, ALU.subtract).then_inc(s["neg_dt"], 1)

            def make_u(k, h):
                dve.wait_ge(s["neg_dt"], ONE + k + 1)
                dve.wait_ge(s["xn"][h], (k // 2) * 16 + 16)
                dve.wait_ge(s["bx"], ONE + k * NDVE)
                V.scalar_tensor_tensor(u[:, :], neg_dt[:, h, :], -1.0, xn[:, h, :],
                                       ALU.mult, ALU.mult).then_inc(s["u"], 1)

            def step(k, h, first=False, last=False):
                slot = (k // DT) % 2

                def make_input(n):
                    dve.wait_ge(s["scan"], slot_used(k, n))
                    V.tensor_tensor(bx[:, ring_slot(n), :], u[:, :], bc[:, bass.ds(slot, 1), n, :]
                                    .rearrange("p a t -> p (a t)"), ALU.mult).then_inc(s["bx"], 1)

                def scan(n):
                    U = k * S + n
                    if n == 0:
                        dve.wait_ge(s["first"], k + 1)
                        dve.wait_ge(s["state"], k * 2 + 1)
                    if n == HSLOTS:
                        dve.wait_ge(s["state"], k * 2 + 2)
                    dve.wait_ge(s["scaled"], U + 1)
                    dve.wait_ge(s["decay"], U + 1)
                    if n in PE_STATES:
                        dve.wait_ge(s["bx_pe"], ONE + k * NPE + PE_STATES.index(n) + 1)
                        factor, addend = decay_sb[:, :], bx_pe[:, :]
                    else:
                        dve.wait_ge(s["bx"], ONE + k * NDVE + DVE_STATES.index(n) + 1)
                        factor, addend = decay[ring_slot(n)][:, :], bx[:, ring_slot(n), :]
                    V.tensor_tensor_scan(hs[:, n % HSLOTS, :], factor, addend,
                                         h_first[:, h, n:n + 1], ALU.mult, ALU.add).then_inc(s["scan"], 1)

                def save(k, half):
                    dve.wait_ge(s["scan"], SCAN_CREDIT + k * S + (half + 1) * HSLOTS)
                    V.tensor_scalar(h_last[:, bass.ds(k % DT, 1), half * HSLOTS:(half + 1) * HSLOTS],
                                    hs[:, :, T - 1].unsqueeze(1), 1.0, None, ALU.mult).then_inc(s["state"], 1)

                dve.wait_ge(s["b"], (k // DT + 1) * B_LOADS)
                dve.wait_ge(s["u_in"], ONE + k + 1)
                make_input(0)
                if not first:
                    save(k - 1, 1)
                make_input(1)
                for n in range(S):
                    if n >= 1 and n + 1 in DVE_STATES and n != 10:
                        make_input(n + 1)
                    if n == HSLOTS:
                        save(k, 0)
                        make_input(11)
                    if n == S - 3 and not last:
                        make_neg_dt(k + 1, 1 - h)
                    if n == S - 2 and not last:
                        make_u(k + 1, 1 - h)
                    scan(n)

            make_neg_dt(0, 0)
            make_u(0, 0)
            step(0, 0, first=True)
            with dve.Fori(0, (K - 2) // 2, 1) as i:
                step(i * 2 + 1, 1)
                step(i * 2 + 2, 0)
            step(K - 1, 1, last=True)

        @block.gpsimd
        def _(pool):
            pool.sem_inc(s["scaled"], HSLOTS)
            pool.wait_ge(s["const"], 32)

            def make_b_diag(c):
                k = c * DT
                pool.wait_ge(s["b"], (c + 1) * B_LOADS)
                for j, n in enumerate(PE_STATES):
                    POOL.tensor_tensor(
                        b_diag[:, bass.ds((k // DT) % 2, 1), j, :, :].rearrange("p o a t -> p (o a) t"),
                        bc[:, bass.ds((k // DT) % 2, 1), n, :].rearrange("p o (a t) -> p (o a) t", t=P),
                        bcast(ident[:, :].unsqueeze(1), [P, T // P, P]), ALU.mult).then_inc(s["b_diag"], 1)

            def products(c, begin, end):
                with pool.Fori(begin // 2, end // 2, 1) as i:
                    for h in range(2):
                        k = c * DT + i * 2 + h
                        for n in range(S):
                            U = k * S + n
                            if h == 0 and n == 0:
                                pool.wait_ge(s["chunk"], (c + 1) * C_LOADS)
                            pool.wait_ge(s["summed"], U + 1)
                            pool.wait_ge(s["scan"], SCAN_CREDIT + U + 1)
                            POOL.tensor_tensor(ch[:, n % GSLOTS, :], hs[:, n % HSLOTS, :],
                                               bc[:, bass.ds((k // DT) % 2, 1), S + n, :]
                                               .rearrange("p a t -> p (a t)"), ALU.mult).then_inc(s["scaled"], 1)

            make_b_diag(0)
            with pool.Fori(0, CHUNKS - 1, 1) as c:
                products(c, 0, DT - 4)
                pool.wait_ge(s["bx_pe"], ONE + c * DT * NPE)
                make_b_diag(c + 1)
                products(c, DT - 4, DT)
            products(CHUNKS - 1, 0, DT)

        @block.tensor
        def _(pe):
            pe.sem_inc(s["summed"], GSLOTS)
            pe.sem_inc(s["turned"], TWO)
            pe.sem_inc(s["skip"], TWO)
            pe.sem_inc(s["u_turned"], ONE)
            pe.sem_inc(s["bx_pe"], ONE)
            pe.wait_ge(s["const"], 32)

            def raw_dt(k, h):
                pe.wait_ge(s["params"][h], (k // 2) * 32 + 32)
                pe.wait_ge(s["chunk"], (k // DT + 1) * C_LOADS)
                PE.matmul(dt_raw[:, :], wdt[:, h, :], dt_in[:, bass.ds((k // DT) % 2, 1), :]
                          .rearrange("p a t -> p (a t)"), start=True, stop=True).then_inc(s["dt_raw"], 1)

            def turn_u(k):
                pe.wait_ge(s["u_in"], ONE + k + 1)
                for a in range(T // P):
                    mm = PE.transpose(turned_u[:, a * P:(a + 1) * P], u_sb[:, a * P:(a + 1) * P], ident[:, :])
                mm.then_inc(s["u_turned"], 1)

            def make_input(k, n):
                pe.wait_ge(s["b_diag"], (k // DT + 1) * NPE)
                pe.wait_ge(s["u_time"], k + 1)
                pe.wait_ge(s["scan"], pe_used(k, n))
                for a in range(T // P):
                    mm = PE.matmul(bx_pe[:, a * P:(a + 1) * P], u_time[:, a, :],
                                   b_diag[:, bass.ds((k // DT) % 2, 1), PE_STATES.index(n), a, :]
                                   .rearrange("p o t -> p (o t)"), start=True, stop=True)
                mm.then_inc(s["bx_pe"], 1)

            def turn(k, h):
                pe.wait_ge(s["y_in"], ONE + k + 1)
                pe.wait_ge(s["x_blk"][h], (k // 2) * 16 + 16)
                PE.matmul(turned[:, :], ident[:, :], x_blk[:, h, :, :].rearrange("p a c -> p (a c)"),
                          start=True, stop=False)
                for a in range(T // P):
                    mm = PE.matmul(turned[:, a * P:(a + 1) * P], y_sb[:, a * P:(a + 1) * P], ident[:, :],
                                   start=False, stop=(a == T // P - 1))
                mm.then_inc(s["turned"], 1)

            def step(k, h, first=False, last=False):
                pe.wait_ge(s["diag"], TWO + k + 1)
                pe.wait_ge(s["u"], k + 1)
                pe.wait_ge(s["xn"][h], (k // 2) * 16 + 16)
                if not first:
                    pe.wait_ge(s["y_in"], k)
                PE.matmul(acc[h][:, :], diag_d[:, h, :], xn[:, h, :], start=True,
                          stop=False).then_inc(s["skip"], 1)
                for n in range(S):
                    pe.wait_ge(s["scaled"], HSLOTS + k * S + n + 1)
                    mm = PE.matmul(acc[h][:, :], ident[:, :], ch[:, n % GSLOTS, :],
                                   start=False, stop=(n == S - 1))
                    mm.then_inc(s["summed"], 1)
                    if n + 5 in PE_STATES:
                        make_input(k, n + 5)
                    if n == 3 and not last:
                        pe.wait_ge(s["u_time"], k + 1)
                        raw_dt(k + 1, 1 - h)
                    if n == 7 and not first:
                        if last:
                            pe.wait_ge(s["u_time"], k + 1)
                        else:
                            pe.wait_ge(s["dt_read"], k + 2)
                        turn(k - 1, 1 - h)
                    if n == 14 and not last:
                        if first:
                            pe.wait_ge(s["dt_read"], k + 2)
                        else:
                            pe.wait_ge(s["turned_in"], k)
                        turn_u(k + 1)

            raw_dt(0, 0)
            pe.wait_ge(s["dt_read"], 1)
            turn_u(0)
            step(0, 0, first=True)
            with pe.Fori(0, (K - 2) // 2, 1) as i:
                step(i * 2 + 1, 1)
                step(i * 2 + 2, 0)
            step(K - 1, 1, last=True)
            pe.wait_ge(s["turned_in"], K - 1)
            turn(K - 1, 1)


SCAN_SIGNALS = ["const", "chunk", "b", "b_diag", "u_in", "u_turned", "u_time", "bx_pe", "turned", "dt_read", "y_in", "turned_in", "neg_a", "dt_raw", "soft",
                "neg_dt", "scan", "decay", "state", "first", "skip", "diag", "bx", "u", "scaled", "summed"]


def build(nc, x, w_logit, base, gate, w_branch, w_proj, channels, w_dt, consts, keep, out):
    def scratch(name, shape):
        return nc.dram_tensor(name, shape, F32, kind="Internal").ap()

    x1, x2 = (scratch(n, [TOKENS * STREAMS, W]) for n in ("x1", "x2"))
    normed = scratch("normed", [K * P, T])
    projected = scratch("projected", [NP, TOKENS])
    with ExitStack() as ctx:
        ffn1, ffn2 = (signals(nc, ctx, n, FFN_SIGNALS, ("stored", "loaded", "again")) for n in ("ffn1", "ffn2"))
        project = signals(nc, ctx, "project", PROJECT_SIGNALS, ("stored", "loaded"))
        scan = signals(nc, ctx, "scan", SCAN_SIGNALS, ("stored", "params", "xn", "x_blk"))
        ffn_program(nc, "ffn1", ffn1, x, x1, consts, w_logit, base, gate, w_branch)
        project_program(nc, "project", project, x1, normed, projected, consts, w_proj)
        scan_program(nc, "scan", scan, x1, normed, projected, x2, consts, channels, w_dt, keep)
        ffn_program(nc, "ffn2", ffn2, x2, out, consts, w_logit, base, gate, w_branch)


def constants():
    import numpy as np
    p = np.arange(P)
    c = np.zeros((P, C_COLS), np.float32)
    c[:, C_IDENT:C_IDENT + P] = p[:, None] == p[None, :]
    for q in range(Q):
        c[:, C_SEL + q * P:C_SEL + (q + 1) * P] = p[:, None] == q * TPR + p[None, :] // STREAMS
    c[:, C_STREAM:C_STREAM + STREAMS] = p[:, None] % STREAMS == np.arange(STREAMS)
    c[:, C_TOKEN:C_TOKEN + TPR] = p[:, None] // STREAMS == np.arange(TPR)
    c[:, C_HALF:C_SEL] = -0.5
    keep = np.ones((P, K), np.float32)
    keep[:, np.arange(K) // DT % CPB == 0] = 0.0
    return c, keep


def kernel(L0_attn_x, L0_attn_A_log, L0_attn_D, L0_attn_x_proj_w, L0_attn_dt_proj_w, L0_attn_dt_proj_b,
           L0_ffn_W_res, L0_ffn_W_pre, L0_ffn_W_post, L0_ffn_H_res_base, L0_ffn_H_pre_base,
           L0_ffn_H_post_base, L0_ffn_gate, L0_ffn_W_branch):
    import numpy as np
    import concourse.bacc as bacc
    from concourse.bass_utils import run_bass_kernel_spmd

    def tiles(w):
        return np.ascontiguousarray(w.T.reshape(-1, P, w.shape[0]).transpose(1, 0, 2))

    consts, keep = constants()
    arrays = {
        "x": np.ascontiguousarray(L0_attn_x).reshape(TOKENS * STREAMS, W),
        "w_logit": tiles(np.concatenate([L0_ffn_W_res, L0_ffn_W_pre, L0_ffn_W_post])),
        "base": np.concatenate([np.asarray(L0_ffn_H_res_base).reshape(-1), L0_ffn_H_pre_base, L0_ffn_H_post_base]),
        "gate": np.ascontiguousarray(L0_ffn_gate),
        "w_branch": np.ascontiguousarray(np.asarray(L0_ffn_W_branch).reshape(KB, P, W).transpose(1, 0, 2)),
        "w_proj": tiles(np.asarray(L0_attn_x_proj_w)),
        "channels": np.concatenate([L0_attn_A_log, np.asarray(L0_attn_D)[:, None],
                                    np.asarray(L0_attn_dt_proj_b)[:, None]], axis=1),
        "w_dt": np.ascontiguousarray(np.asarray(L0_attn_dt_proj_w).reshape(DT, P, RANK)
                                     .transpose(0, 2, 1)).reshape(DT * RANK, P),
        "consts": consts,
        "keep": keep,
    }
    nc = bacc.Bacc("TRN2", target_bir_lowering=False, num_devices=1)
    aps = {n: nc.dram_tensor(f"{n}_dram", a.shape, F32, kind="ExternalInput").ap() for n, a in arrays.items()}
    out = nc.dram_tensor("out_dram", [TOKENS * STREAMS, W], F32, kind="ExternalOutput").ap()
    build(nc, **aps, out=out)
    r = run_bass_kernel_spmd(nc, [{f"{n}_dram": a for n, a in arrays.items()}], core_ids=[0])
    return r.results[0]["out_dram"].reshape(BATCH, SEQ, D)
```
